# Optimizing a Trainium2 kernel written in Bass

```python
import numpy as np
import jax
import jax.numpy as jnp

def _softmax(x, axis=-1):
    return jax.nn.softmax(x, axis=axis)

def _gelu(x):
    return jax.nn.gelu(x, approximate=True)

def _silu(x):
    return jax.nn.silu(x)

def _sigmoid(x):
    return jax.nn.sigmoid(x)

def _layernorm(x, axis=-1, eps=1e-05):
    m = jnp.mean(x, axis=axis, keepdims=True)
    v = jnp.var(x, axis=axis, keepdims=True)
    return (x - m) / jnp.sqrt(v + eps)

def _scatter_add(tgt, idx, src, axis=0):
    return tgt.at[idx].add(src)

def _segment_sum(src, seg, n):
    return jax.ops.segment_sum(src, seg, n)
kernel_name = 'mk_adj_preln_d1_adj_r2_611691'

def setup_inputs(seed: int=0):
    np.random.seed(seed)
    _w = jnp.asarray

    def _rec_inputs():
        import jax
        import jax.numpy as jnp
        _gk = jax.random.key(seed)
        x = -0.0002928 + 1 * jax.random.normal(jax.random.fold_in(_gk, 1), (8192, 256), jnp.float32)
        _w = (1.0 + jnp.arange(8192, dtype=jnp.float32)) ** (-0.5)
        _w = _w / _w.mean()
        _pij = jnp.clip(0.00195312 * _w[:, None] * _w[None, :], 0.0, 1.0)
        _a = jax.random.uniform(jax.random.fold_in(_gk, 2), (8192, 8192)) < _pij
        adj = _a.astype(jnp.int32)
        return (x, adj)
    x, adj = _rec_inputs()

    def _L0_gnn_setup():
        import jax, jax.numpy as jnp
        import numpy as np
        N = 4096
        IN_F = 256
        OUT_F = 256
        ALPHA = 0.2
        key = jax.random.key(seed)
        k1, k2, k3, k4, k5 = jax.random.split(key, 5)
        inp = jax.random.normal(k1, (N, IN_F), dtype=jnp.float32)
        adj = jax.random.randint(k2, (N, N), 0, 2, dtype=jnp.int32)
        W1 = jax.random.normal(k3, (IN_F, OUT_F), dtype=jnp.float32) * (1.0 / np.sqrt(IN_F))
        b1 = jnp.zeros((OUT_F,), dtype=jnp.float32)
        a = jax.random.normal(k4, (2 * OUT_F,), dtype=jnp.float32) * (1.0 / np.sqrt(2 * OUT_F))
        a1 = a[:OUT_F]
        a2 = a[OUT_F:]
        b2 = jnp.zeros((), dtype=jnp.float32)
        return {'inp': inp, 'adj': adj, 'W1': W1, 'b1': b1, 'a1': a1, 'a2': a2, 'b2': b2}
    _L0_gnn_all = _L0_gnn_setup()
    _L0_gnn_in = {k: v for k, v in _L0_gnn_all.items() if k in ('W1', 'b1', 'a1', 'a2', 'b2')}
    del _L0_gnn_all
    return {'x': x, 'adj': adj, 'L0_gnn_W1': _L0_gnn_in['W1'], 'L0_gnn_b1': _L0_gnn_in['b1'], 'L0_gnn_a1': _L0_gnn_in['a1'], 'L0_gnn_a2': _L0_gnn_in['a2'], 'L0_gnn_b2': _L0_gnn_in['b2']}

def reference(x, adj, L0_gnn_W1, L0_gnn_b1, L0_gnn_a1, L0_gnn_a2, L0_gnn_b2):
    import jax
    import jax.numpy as jnp

    def _L0_gnn_ref(inp, adj, W1, b1, a1, a2, b2):
        import jax, jax.numpy as jnp
        import numpy as np
        N = 4096
        IN_F = 256
        OUT_F = 256
        ALPHA = 0.2
        h = inp @ W1 + b1
        e = jax.nn.leaky_relu((h @ a1)[:, None] + (h @ a2)[None, :] + b2, ALPHA)
        attention = jnp.where(adj > 0, e, jnp.float32(-1000000000000.0))
        attention = jax.nn.softmax(attention, axis=1)
        h_prime = attention @ h
        return jax.nn.elu(h_prime)
    h = jnp.maximum(_layernorm(x, axis=-1), 0.0)
    x = x + _L0_gnn_ref(h, adj, L0_gnn_W1, L0_gnn_b1, L0_gnn_a1, L0_gnn_a2, L0_gnn_b2)
    return x

_drawn_inputs = setup_inputs


def setup_inputs(seed=0):
    import zlib

    import numpy as np

    out = dict(_drawn_inputs(seed))
    spreads = {'L0_gnn_b1': (0.0, 0.1)}
    factors = {'L0_gnn_a1': 28.883}
    for name, (base, spread) in spreads.items():
        noise = np.random.default_rng([zlib.crc32(name.encode()), seed]).standard_normal(out[name].shape)
        drawn = base * np.exp(spread * noise) if base else spread * noise
        out[name] = jnp.asarray(drawn.astype(out[name].dtype))
    for name, factor in factors.items():
        out[name] = (out[name] * factor).astype(out[name].dtype)
    return out
```

```python
from contextlib import ExitStack

import concourse.bass as bass
from concourse import mybir

F32 = mybir.dt.float32
F16 = mybir.dt.float16
F8 = mybir.dt.float8e4
I32 = mybir.dt.int32
U32 = mybir.dt.uint32
ALU = mybir.AluOpType
ACT = mybir.ActivationFunctionType
AX_X = mybir.AxisListType.X
RMAX = bass.bass_isa.ReduceOp.max

P = 128
QUADS = 4
R = P // QUADS
ALPHA = 0.2
EPS = 1e-5
PLUS, MINUS = 0, 1
HIGH, LOW = 0, 1
LOW_SCALE = 4096.0
TABLE_SHIFT = 8.0 * 0.6931471805599453
HUGE = 3.0e38


def adjacency_attention(nc, x, adj, w1, b1, a1, a2, b2, out):
    N, F = x.shape
    QN = N // QUADS
    CH = QN // R
    TILES = CH
    FD = F + 1
    FE = F + 2
    KK = F // P
    PIECES = 2
    PW = QN // PIECES
    PACK = 4
    PB = PW // (R * PACK)
    PCH = PW // R
    SLOTS = 8
    GX = 8
    TB = 4

    x_rows = x.rearrange("(g n) f -> g n f", g=QUADS)
    out_rows = out.rearrange("(g n) f -> g n f", g=QUADS)
    adj_rows = adj.rearrange("(g n) (q j) -> g n q j", g=QUADS, q=QUADS)

    ctx = ExitStack()
    with ctx:
        def sb(name, shape, dt):
            return ctx.enter_context(nc.sbuf_tensor(name, shape, dt))

        def sem(name):
            return ctx.enter_context(nc.semaphore(name))

        tables = sb("tables", [P, 2, CH, 2, FE], F16)
        h32 = tables[:, PLUS, :, :, :].rearrange("p m a f -> p m (a f)").bitcast(F32)
        adj_ring = sb("adj_ring", [P, SLOTS, PW], I32)
        tau = sb("tau", [P, 2, QN], F32)
        work = sb("work", [P, 6 * 1024], F32)
        workb = work[:, :].bitcast(F8)
        masks = workb[:, 0:2 * 4 * PW].rearrange("p (c g w e) -> p c g w e", c=2, g=QUADS, e=PACK)
        turned = workb[:, 8 * PW:24 * PW].rearrange("p (s c b i e) -> p s c b i e", s=2, c=2, b=PB, e=PACK)
        xs = work[:, 0:GX * F].rearrange("p (k f) -> p k f", k=GX)
        hn = work[:, 2048:2048 + 2 * F].rearrange("p (k f) -> p k f", k=2)
        hnT = work[:, 2560:2560 + 2 * F].rearrange("p (k a i) -> p k a i", k=2, a=KK)
        w1_sb = work[:, 3072:3072 + KK * FE].rearrange("p (a f) -> p a f", a=KK)
        a_bc = work[:, 3600:3600 + 2 * F].rearrange("p (a f) -> p a f", a=2)
        b_bc = work[:, 4112:4112 + FE]
        ident = work[:, 4384:4384 + P]
        pick = work[:, 4512:4512 + QUADS * P].rearrange("p (g q r) -> p g q r", g=QUADS, q=QUADS)
        quad_ones = work[:, 5024:5024 + P]
        all_ones = work[:, 5152:5152 + P]
        eye32 = work[:, 5280:5280 + R]
        junk = work[:, 5312:5312 + F]
        spread = work[:, 0:QN].rearrange("p (m c) -> p m c", c=R)
        scaled = work[:, 0:4 * TB * F].rearrange("p (s c k f) -> p s c k f", s=2, c=2, k=TB)

        stats = sb("stats", [P, GX, 6], F32)
        mv = sb("mv", [P, GX, 2], F32)
        sd = sb("sd", [P, GX], F32)
        rstd = sb("rstd", [P, GX], F32)
        shift = sb("shift", [P, GX], F32)
        st = sb("st", [P, CH, 2], F32)
        hsum = sb("hsum", [P, F], F32)
        hmean = sb("hmean", [P, F], F32)
        b2_bc = sb("b2_bc", [P, 1], F32)
        eps_col = sb("eps_col", [P, 1], F32)
        ends = sb("ends", [P, 2], F32)
        span = sb("span", [P, 2], F32)
        k0 = sb("k0", [P, 1], F32)
        k1 = sb("k1", [P, 1], F32)
        k2 = sb("k2", [P, 1], F32)
        ebias = sb("ebias", [P, 2], F32)
        grid = sb("grid", [P, 2, CH], F32)
        grid2 = sb("grid2", [P, 2, CH], F32)
        psi = sb("psi", [P, 2, QUADS, TILES], F32)
        psi_now = sb("psi_now", [P, 2, QUADS], F32)
        z = sb("z", [P, CH], F32)
        gamma = sb("gamma", [P, CH], F32)
        gamma_low = sb("gamma_low", [P, CH], F32)
        fac = sb("fac", [P, 2, CH], F32)
        fac_low = sb("fac_low", [P, 2, CH], F32)
        parts = sb("parts", [P, 4, FE], F32)
        xt = sb("xt", [P, F], F32)
        flag = sb("flag", [P, 1], F32)
        den = sb("den", [P, 1], F32)
        rden = sb("rden", [P, 1], F32)
        num = sb("num", [P, F], F32)
        neg = sb("neg", [P, F], F32)
        pos = sb("pos", [P, F], F32)
        ot = sb("ot", [P, F], F32)

        acc = [[[ctx.enter_context(nc.psum_tensor(f"acc{b}{c}{a}", [P, 512], F32)) for a in range(2)]
                for c in range(2)] for b in range(2)]
        bank = [acc[b][c][a] for b in range(2) for c in range(2) for a in range(2)]

        s_const = sem("s_const")
        s_eye = sem("s_eye")
        s_x = [sem(f"s_x{k}") for k in range(GX)]
        s_norm = sem("s_norm")
        s_var = sem("s_var")
        s_sd = sem("s_sd")
        s_rs = sem("s_rs")
        s_tp = sem("s_tp")
        s_tc = sem("s_tc")
        s_hp = sem("s_hp")
        s_h = sem("s_h")
        s_w = sem("s_w")
        s_hs = sem("s_hs")
        s_mean = sem("s_mean")
        s_ends = sem("s_ends")
        s_span = sem("s_span")
        s_spread = sem("s_spread")
        s_bc = sem("s_bc")
        s_thr = sem("s_thr")
        s_eb = sem("s_eb")
        s_exp = sem("s_exp")
        s_fac = sem("s_fac")
        s_scx = sem("s_scx")
        s_scy = sem("s_scy")
        s_hi = sem("s_hi")
        s_lo = sem("s_lo")
        s_adj = [sem(f"s_adj{k}") for k in range(SLOTS)]
        s_mask = sem("s_mask")
        s_psi = sem("s_psi")
        s_turn = sem("s_turn")
        s_mm = sem("s_mm")
        s_xt = sem("s_xt")
        s_copy = sem("s_copy")
        s_sum = sem("s_sum")
        s_neg = sem("s_neg")
        s_elu = sem("s_elu")
        s_res = sem("s_res")
        s_ot = sem("s_ot")
        s_out = sem("s_out")
        s_passed = sem("s_passed")
        s_dve = sem("s_dve")

        def wait_alone(eng, semaphore, value):
            eng.wait_ge(semaphore, value)
            eng.sem_inc(s_passed, 1)

        block = ctx.enter_context(nc.Block())

        @block.sync
        def _(sp):
            sp.dma_start(w1_sb[:, :, 0:F], w1.rearrange("(a k) f -> k a f", a=KK)).then_inc(s_const, 16)
            sp.dma_start(a_bc[:, 0, :], a1.rearrange("(o f) -> o f", o=1).broadcast_to((P, F))).then_inc(s_const, 16)
            sp.dma_start(a_bc[:, 1, :], a2.rearrange("(o f) -> o f", o=1).broadcast_to((P, F))).then_inc(s_const, 16)
            sp.dma_start(b_bc[:, 0:F], b1.rearrange("(o f) -> o f", o=1).broadcast_to((P, F))).then_inc(s_const, 16)
            sp.dma_start(b2_bc[:, :], b2.rearrange("(o f) -> o f", o=1).broadcast_to((P, 1))).then_inc(s_const, 16)
            for k in range(GX):
                sp.dma_start(xs[:, k, :], x_rows[:, k * R:(k + 1) * R, :]).then_inc(s_x[k], 16)
            with sp.Fori(0, CH // GX - 1) as u:
                for k in range(GX):
                    sp.wait_ge(s_norm, u * GX + (k + 1))
                    sp.dma_start(xs[:, k, :], x_rows[:, bass.ds(u * (GX * R) + (GX + k) * R, R), :]).then_inc(s_x[k], 16)

            def load(row0, w, g):
                sp.dma_start(adj_ring[:, 4 * w + g, :],
                             adj_rows[g, row0, :, w * PW:(w + 1) * PW].rearrange("r q j -> q r j"))\
                  .then_inc(s_adj[4 * w + g], 16)

            for w in range(PIECES):
                for g in range(QUADS):
                    load(slice(0, R), w, g)
            with sp.Fori(0, TILES - 1) as n:
                for w in range(PIECES):
                    for g in range(QUADS):
                        sp.wait_ge(s_mask, n * (8 * PIECES) + (8 * w + 4 + g + 1))
                        load(bass.ds(n * R + R, R), w, g)

        @block.gpsimd
        def _(pool):
            step = [0]

            def done(ins):
                step[0] += 1
                ins.then_inc(s_eye, 1)
                pool.wait_ge(s_eye, step[0])

            done(nc.gpsimd.memset(work[:, 4384:5312], 0.0))
            done(nc.gpsimd.memset(all_ones, 1.0))
            done(nc.gpsimd.affine_select(out=ident, in_=ident, compare_op=ALU.not_equal, fill=1.0, base=0,
                                         pattern=[[-1, P]], channel_multiplier=1))
            for g in range(QUADS):
                done(nc.gpsimd.affine_select(out=pick[:, g, :, :], in_=pick[:, g, :, :], compare_op=ALU.not_equal,
                                             fill=1.0, base=-R * g, pattern=[[0, QUADS], [-1, R]],
                                             channel_multiplier=1))
            for g in range(QUADS):
                done(nc.gpsimd.affine_select(out=eye32, in_=eye32, compare_op=ALU.not_equal, fill=1.0, base=-R * g,
                                             pattern=[[-1, R]], channel_multiplier=1))
            for q in range(QUADS):
                done(nc.gpsimd.memset(quad_ones[R * q:R * q + R, R * q:R * q + R], 1.0))
            done(nc.gpsimd.memset(hsum[:, :], 0.0))
            pool.wait_ge(s_h, 1)
            nc.gpsimd.tensor_tensor(hsum[:, :], hsum[:, :], h32[:, 0, 0:F], ALU.add).then_inc(s_hs, 1)
            with pool.Fori(1, CH) as m:
                pool.wait_ge(s_h, m + 1)
                pool.wait_ge(s_hs, m)
                nc.gpsimd.tensor_tensor(hsum[:, :], hsum[:, :], h32[:, m, 0:F], ALU.add).then_inc(s_hs, 1)
            pool.wait_ge(s_ends, 1)
            nc.gpsimd.partition_all_reduce(span[:, :], ends[:, :], P, RMAX).then_inc(s_span, 1)

            with pool.Fori(0, TILES) as n:
                pool.wait_ge(s_copy, n + 1)
                nc.gpsimd.tensor_tensor(parts[:, 0, 0:FD], parts[:, 0, 0:FD], parts[:, 1, 0:FD], ALU.add).then_inc(s_sum, 1)
                nc.gpsimd.tensor_tensor(parts[:, 2, 0:FD], parts[:, 2, 0:FD], parts[:, 3, 0:FD], ALU.add).then_inc(s_sum, 1)
                pool.wait_ge(s_sum, n * 3 + 2)
                nc.gpsimd.tensor_tensor(parts[:, 0, 0:FD], parts[:, 0, 0:FD], parts[:, 2, 0:FD], ALU.add).then_inc(s_sum, 1)
                pool.wait_ge(s_elu, n + 1)
                pool.wait_ge(s_xt, n * 16 + 16)
                nc.gpsimd.tensor_tensor(pos[:, :], pos[:, :], xt[:, :], ALU.add).then_inc(s_res, 1)

        @block.scalar
        def _(act):
            act.wait_ge(s_dve, 1)
            def normalise(u, first):
                act.wait_ge(s_var, u + 1)
                nc.scalar.activation(sd[:, :], mv[:, :, 1], ACT.Sqrt, bias=eps_col[:, :]).then_inc(s_sd, 1)
                act.wait_ge(s_rs, u + 1)
                for k in range(GX + 1):
                    if k < GX:
                        act.wait_ge(s_x[k], u * 16 + 16)
                        if k >= 2:
                            act.wait_ge(s_tp, u * GX + (k - 1))
                        nc.scalar.activation(hn[:, k % 2, :], xs[:, k, :], ACT.Relu, scale=rstd[:, k:k + 1],
                                             bias=shift[:, k:k + 1]).then_inc(s_norm, 1)
                    if k >= 1:
                        c = k - 1
                        act.wait_ge(s_tp, u * GX + (c + 1))
                        if c >= 2 or not first:
                            act.wait_ge(s_hp, u * GX + max(c - 1, 0))
                        nc.scalar.activation(hnT[:, c % 2, :, :],
                                             bank[c % 2][:, 0:F].rearrange("p (a i) -> p a i", a=KK),
                                             ACT.Copy).then_inc(s_tc, 1)

            normalise(0, True)
            with act.Fori(1, CH // GX) as u:
                normalise(u, False)

            act.wait_ge(s_eb, 1)
            nc.scalar.activation(gamma[:, :], z[:, :], ACT.Exp, scale=-(1.0 - ALPHA))
            nc.scalar.activation(fac[:, PLUS, :], st[:, :, 1], ACT.Exp, bias=ebias[:, 0:1])
            nc.scalar.activation(fac[:, MINUS, :], st[:, :, 1], ACT.Exp, bias=ebias[:, 1:2], scale=ALPHA).then_inc(s_exp, 1)

            act.wait_ge(s_fac, 1)
            STEPS = CH // TB

            def table_step(m0, slot, j, free):
                if free is not None:
                    act.wait_ge(s_lo, free)
                for k in range(TB):
                    last = nc.scalar.activation(scaled[:, slot, MINUS, k, :], h32[:, m0 + k, 0:F], ACT.Copy,
                                                scale=fac_low[:, MINUS, bass.ds(m0 + k, 1)])
                last.then_inc(s_scy, 1)
                act.wait_ge(s_scy, j + 1)
                nc.scalar.activation(tables[:, MINUS, bass.ds(m0, TB), HIGH, 0:F], scaled[:, slot, MINUS, :, :], ACT.Copy,
                                     scale=1.0 / LOW_SCALE).then_inc(s_hi, 1)
                act.wait_ge(s_scx, j + 1)
                nc.scalar.activation(tables[:, PLUS, bass.ds(m0, TB), HIGH, 0:F], scaled[:, slot, PLUS, :, :], ACT.Copy,
                                     scale=1.0 / LOW_SCALE).then_inc(s_hi, 1)

            for slot in range(2):
                table_step(slot * TB, slot, slot, None)
            with act.Fori(1, STEPS // 2) as v:
                for slot in range(2):
                    table_step(v * (2 * TB) + slot * TB, slot, v * 2 + slot, v * 4 + (2 * slot - 2))

            act.wait_ge(s_lo, 2 * STEPS)
            for c in range(2):
                last = nc.scalar.activation(tables[:, c, :, HIGH, F], fac[:, c, :], ACT.Copy)
            last.then_inc(s_hi, 1)

            act.dma_start(xt[:, :], x_rows[:, 0:R, :]).then_inc(s_xt, 16)

            def tile_end(n, b, before):
                act.wait_ge(s_mm, n * PIECES + PIECES)
                if before:
                    act.wait_ge(s_ot, n)
                nc.scalar.activation(parts[:, 0, 0:FD], acc[b][PLUS][HIGH][:, 0:FD], ACT.Copy)
                nc.scalar.activation(parts[:, 1, 0:FD], acc[b][PLUS][LOW][:, 0:FD], ACT.Copy, scale=1.0 / LOW_SCALE)
                nc.scalar.activation(parts[:, 2, 0:FD], acc[b][MINUS][HIGH][:, 0:FD], ACT.Copy, scale=gamma[:, bass.ds(n, 1)])
                nc.scalar.activation(parts[:, 3, 0:FD], acc[b][MINUS][LOW][:, 0:FD], ACT.Copy,
                                     scale=gamma_low[:, bass.ds(n, 1)]).then_inc(s_copy, 1)
                act.wait_ge(s_neg, n + 1)
                nc.scalar.activation(pos[:, :], num[:, :], ACT.Relu, scale=rden[:, :])
                nc.scalar.activation(neg[:, :], neg[:, :], ACT.Exp).then_inc(s_elu, 1)
                act.wait_ge(s_ot, n + 1)
                act.dma_start(out_rows[:, bass.ds(n * R, R), :], ot[:, :]).then_inc(s_out, 16)

            def next_x(n):
                act.wait_ge(s_res, n + 1)
                act.dma_start(xt[:, :], x_rows[:, bass.ds(n * R + R, R), :]).then_inc(s_xt, 16)

            tile_end(0, 0, False)
            next_x(0)
            tile_end(1, 1, True)
            with act.Fori(1, TILES // 2) as v:
                for b in range(2):
                    next_x(v * 2 + (b - 1))
                    tile_end(v * 2 + b, b, True)
            act.wait_ge(s_out, 16 * TILES)

        @block.vector
        def _(dve):
            chain = [0]

            def link(ins):
                chain[0] += 1
                ins.then_inc(s_dve, 1)
                dve.wait_ge(s_dve, chain[0])

            link(nc.vector.memset(eps_col[:, :], EPS))
            dve.wait_ge(s_const, 80)
            for c in range(2):
                for a in range(KK):
                    link(nc.vector.scalar_tensor_tensor(out=junk, in0=w1_sb[:, a, 0:F], scalar=1.0, in1=a_bc[:, c, :],
                                                        op0=ALU.mult, op1=ALU.mult,
                                                        accum_out=w1_sb[:, a, F + c:F + c + 1]))
                link(nc.vector.scalar_tensor_tensor(out=junk, in0=b_bc[:, 0:F], scalar=1.0, in1=a_bc[:, c, :],
                                                    op0=ALU.mult, op1=ALU.mult, accum_out=b_bc[:, F + c:F + c + 1]))
            nc.vector.tensor_tensor(b_bc[:, F:F + 1], b_bc[:, F:F + 1], b2_bc[:, :], ALU.add).then_inc(s_w, 1)
            dve.wait_ge(s_w, 1)

            C0 = chain[0]
            with dve.Fori(0, CH // GX) as u:
                for k in range(GX):
                    dve.wait_ge(s_x[k], u * 16 + 16)
                    nc.vector.bn_stats(stats[:, k, :], xs[:, k, :]).then_inc(s_dve, 1)
                wait_alone(dve, s_dve, u * (2 * GX) + (C0 + GX))
                for k in range(GX):
                    last = nc.vector.bn_aggr(mv[:, k, :], stats[:, k, :])
                    if k == GX - 1:
                        last.then_inc(s_var, 1)
                    else:
                        last.then_inc(s_dve, 1)
                dve.wait_ge(s_sd, u + 1)
                nc.vector.reciprocal(rstd[:, :], sd[:, :]).then_inc(s_dve, 1)
                dve.wait_ge(s_dve, u * (2 * GX) + (C0 + 2 * GX))
                nc.vector.scalar_tensor_tensor(out=shift[:, :], in0=mv[:, :, 0], scalar=-1.0, in1=rstd[:, :],
                                               op0=ALU.mult, op1=ALU.mult).then_inc(s_rs, 1)
                for k in range(GX):
                    dve.wait_ge(s_hp, u * GX + (k + 1))
                    nc.vector.tensor_tensor(h32[:, u * GX + k, 0:F], bank[2 + k % 2][:, 0:F], b_bc[:, 0:F], ALU.add)
                    nc.vector.tensor_tensor(st[:, u * GX + k, :], bank[2 + k % 2][:, F:FE], b_bc[:, F:FE], ALU.add).then_inc(s_h, 1)
            chain[0] = C0 + (2 * GX) * (CH // GX)

            dve.wait_ge(s_h, CH)
            link(nc.vector.tensor_reduce(ends[:, 0:1], st[:, :, 1], AX_X, ALU.max))
            link(nc.vector.tensor_reduce(ends[:, 1:2], st[:, :, 1], AX_X, ALU.min))
            nc.vector.tensor_scalar(ends[:, 1:2], ends[:, 1:2], -1.0, None, ALU.mult).then_inc(s_ends, 1)
            dve.wait_ge(s_span, 1)
            link(nc.vector.tensor_tensor(k0[:, :], span[:, 0:1], span[:, 1:2], ALU.add))
            link(nc.vector.tensor_scalar(k1[:, :], k0[:, :], 2.0, 1e-30, ALU.mult, ALU.max))
            link(nc.vector.reciprocal(k2[:, :], k1[:, :]))
            link(nc.vector.tensor_scalar(ebias[:, 0:1], span[:, 0:1], -1.0, TABLE_SHIFT, ALU.mult, ALU.add))
            link(nc.vector.tensor_scalar(ebias[:, 1:2], span[:, 0:1], -ALPHA, TABLE_SHIFT, ALU.mult, ALU.add))
            nc.vector.tensor_scalar(z[:, :], st[:, :, 0], span[:, 0:1], 0.0, ALU.add, ALU.max).then_inc(s_eb, 1)
            link(nc.vector.tensor_scalar(grid[:, 0, :], st[:, :, 0], span[:, 0:1], k2[:, :], ALU.add, ALU.mult))
            link(nc.vector.tensor_scalar(grid2[:, 1, :], st[:, :, 1], -1.0, span[:, 0:1], ALU.mult, ALU.add))
            link(nc.vector.tensor_scalar(grid[:, 1, :], grid2[:, 1, :], k2[:, :], None, ALU.mult))
            link(nc.vector.tensor_scalar(grid2[:, :, :], grid[:, :, :], -0.125, 0.625, ALU.max, ALU.min))
            link(nc.vector.tensor_scalar(grid[:, :, :], grid2[:, :, :], 1.25, -1.0, ALU.add, ALU.add))
            nc.vector.tensor_tensor(spread[:, :, :], grid[:, 1, :].rearrange("p (m o) -> p m o", o=1).broadcast_to((P, CH, R)),
                                         eye32.rearrange("p (o c) -> p o c", o=1).broadcast_to((P, CH, R)), ALU.mult).then_inc(s_spread, 1)
            dve.wait_ge(s_bc, 1)
            for q in range(QN // 512):
                nc.vector.tensor_scalar(tau[:, PLUS, 512 * q:512 * q + 512], bank[q][:, :], 1.0, None, ALU.mult)
                nc.vector.tensor_scalar(tau[:, MINUS, 512 * q:512 * q + 512], bank[q][:, :], -1.0, 1.0, ALU.mult, ALU.add)
            nc.vector.tensor_scalar(psi[:, PLUS, :, :], bank[4][:, 0:QUADS * TILES].rearrange("p (g n) -> p g n", g=QUADS),
                                    1.0, None, ALU.mult)
            nc.vector.tensor_scalar(psi[:, MINUS, :, :], bank[4][:, 0:QUADS * TILES].rearrange("p (g n) -> p g n", g=QUADS),
                                    -1.0, 1.0, ALU.mult, ALU.add)
            nc.vector.tensor_scalar(hmean[:, :], bank[5][:, 0:F], 1.0 / N, None, ALU.mult).then_inc(s_thr, 1)

            dve.wait_ge(s_exp, 1)
            link(nc.vector.tensor_scalar(gamma_low[:, :], gamma[:, :], 1.0 / LOW_SCALE, None, ALU.mult))
            nc.vector.tensor_scalar(fac_low[:, :, :], fac[:, :, :], LOW_SCALE, None, ALU.mult).then_inc(s_fac, 1)
            dve.wait_ge(s_fac, 1)
            STEPS = CH // TB

            def table_scale(m0, slot):
                for k in range(TB):
                    last = nc.vector.tensor_scalar(scaled[:, slot, PLUS, k, :], h32[:, m0 + k, 0:F],
                                                   fac_low[:, PLUS, bass.ds(m0 + k, 1)], None, ALU.mult)
                last.then_inc(s_scx, 1)

            def table_low(m0, slot, j):
                for c, order in ((MINUS, 1), (PLUS, 2)):
                    dve.wait_ge(s_hi, j * 2 + order)
                    nc.vector.scalar_tensor_tensor(out=tables[:, c, bass.ds(m0, TB), LOW, 0:F],
                                                   in0=tables[:, c, bass.ds(m0, TB), HIGH, 0:F], scalar=-LOW_SCALE,
                                                   in1=scaled[:, slot, c, :, :], op0=ALU.mult, op1=ALU.add).then_inc(s_lo, 1)

            def table_pair(v, first):
                if not first:
                    dve.wait_ge(s_lo, v * 4)
                for slot in range(2):
                    table_scale(v * (2 * TB) + slot * TB, slot)
                for slot in range(2):
                    table_low(v * (2 * TB) + slot * TB, slot, v * 2 + slot)

            table_pair(0, True)
            with dve.Fori(1, STEPS // 2) as v:
                table_pair(v, False)
            dve.wait_ge(s_hi, 2 * STEPS + 1)
            for c in range(2):
                last = nc.vector.scalar_tensor_tensor(out=tables[:, c, :, LOW, F], in0=tables[:, c, :, HIGH, F],
                                                      scalar=-LOW_SCALE, in1=fac_low[:, c, :], op0=ALU.mult, op1=ALU.add)
            last.then_inc(s_lo, 1)

            def piece(n, w, turned_before, free):
                for c in range(2):
                    for g in range(QUADS):
                        if g == 0 and turned_before is not None:
                            wait_alone(dve, s_turn, turned_before + c)
                        if c == 0:
                            wait_alone(dve, s_adj[4 * w + g], n * 16 + 16)
                        nc.vector.scalar_tensor_tensor(
                            out=masks[:, c, g, :, :].rearrange("p w e -> p e w"),
                            in0=adj_ring[:, 4 * w + g, :].rearrange("p (e w) -> p e w", e=PACK),
                            scalar=psi_now[:, c, g:g + 1],
                            in1=tau[:, c, w * PW:(w + 1) * PW].rearrange("p (e w) -> p e w", e=PACK),
                            op0=ALU.min, op1=ALU.is_gt if c == PLUS else ALU.is_ge, saturate=False).then_inc(s_mask, 1)
                for c in range(2):
                    dve.wait_ge(s_mask, n * (8 * PIECES) + (8 * w + 4 * c + 4))
                    if free is not None and c == 0:
                        dve.wait_ge(s_mm, free)
                    nc.vector.transpose(
                        turned[:, w, c, :, :, :].rearrange("p b (g r) e -> p g b (r e)", g=QUADS).bitcast(U32),
                        masks[:, c, :, :, :].rearrange("p g (b c) e -> p g b (c e)", b=PB).bitcast(U32)).then_inc(s_turn, 1)

            CT = chain[0]

            def tail_a(n):
                dve.wait_ge(s_sum, n * 3 + 3)
                nc.vector.tensor_scalar(flag[:, :], parts[:, 0, F:FD], 0.0, None, ALU.is_equal).then_inc(s_dve, 1)
                dve.wait_ge(s_dve, n * 4 + (CT + 1))
                nc.vector.tensor_tensor(den[:, :], parts[:, 0, F:FD], flag[:, :], ALU.add).then_inc(s_dve, 1)
                dve.wait_ge(s_dve, n * 4 + (CT + 2))
                nc.vector.reciprocal(rden[:, :], den[:, :]).then_inc(s_dve, 1)
                nc.vector.scalar_tensor_tensor(out=num[:, :], in0=hmean[:, :], scalar=flag[:, :], in1=parts[:, 0, 0:F],
                                               op0=ALU.mult, op1=ALU.add).then_inc(s_dve, 1)
                dve.wait_ge(s_dve, n * 4 + (CT + 4))
                nc.vector.tensor_scalar(neg[:, :], num[:, :], rden[:, :], 0.0, ALU.mult, ALU.min).then_inc(s_neg, 1)

            def tail_b(n, before):
                dve.wait_ge(s_elu, n + 1)
                dve.wait_ge(s_res, n + 1)
                if before:
                    dve.wait_ge(s_out, n * 16)
                nc.vector.scalar_tensor_tensor(out=ot[:, :], in0=neg[:, :], scalar=-1.0, in1=pos[:, :],
                                               op0=ALU.add, op1=ALU.add).then_inc(s_ot, 1)

            def tile(n, first):
                if not first:
                    dve.wait_ge(s_mask, n * (8 * PIECES))
                nc.vector.tensor_copy(psi_now[:, :, :], psi[:, :, :, bass.ds(n, 1)].rearrange("p c g o -> p c (g o)")).then_inc(s_psi, 1)
                dve.wait_ge(s_psi, n + 1)
                piece(n, 0, None if first else n * (2 * PIECES) - 1, None if first else n * PIECES - 1)
                if not first:
                    tail_a(n - 1)
                piece(n, 1, n * (2 * PIECES) + 1, None if first else n * PIECES)

            tile(0, True)
            tile(1, False)
            tail_b(0, False)
            with dve.Fori(2, TILES) as n:
                tile(n, False)
                tail_b(n - 1, True)
            tail_a(TILES - 1)
            tail_b(TILES - 1, True)

        @block.tensor
        def _(pe):
            pe.wait_ge(s_w, 1)
            pe.wait_ge(s_eye, 3 + 2 * QUADS + QUADS + 1)
            def project(u, first):
                for k in range(GX):
                    pe.wait_ge(s_norm, u * GX + (k + 1))
                    if k >= 2 or not first:
                        pe.wait_ge(s_tc, u * GX + max(k - 1, 0))
                    for a in range(KK):
                        last = nc.tensor.transpose(bank[k % 2][:, a * P:(a + 1) * P], hn[:, k % 2, a * P:(a + 1) * P], ident)
                    last.then_inc(s_tp, 1)
                    pe.wait_ge(s_tc, u * GX + (k + 1))
                    if k >= 2:
                        pe.wait_ge(s_h, u * GX + (k - 1))
                    elif not first:
                        pe.wait_ge(s_h, u * GX)
                    for a in range(KK):
                        last = nc.tensor.matmul(bank[2 + k % 2][:, 0:FE], hnT[:, k % 2, a, :], w1_sb[:, a, :],
                                                start=(a == 0), stop=(a == KK - 1))
                    last.then_inc(s_hp, 1)

            project(0, True)
            with pe.Fori(1, CH // GX) as u:
                project(u, False)

            pe.wait_ge(s_hs, CH)
            nc.tensor.matmul(bank[5][:, 0:F], all_ones, hsum[:, :], start=True, stop=True).then_inc(s_mean, 1)
            pe.wait_ge(s_spread, 1)
            for q in range(QN // 512):
                nc.tensor.matmul(bank[q][:, :], quad_ones, work[:, 512 * q:512 * q + 512], start=True, stop=True)
            for g in range(QUADS):
                last = nc.tensor.matmul(bank[4][:, g * TILES:(g + 1) * TILES], pick[:, g, :, :].rearrange("p q r -> p (q r)"),
                                        grid[:, 0, :], start=True, stop=True)
            last.then_inc(s_bc, 1)

            pe.wait_ge(s_lo, 2 * (CH // TB) + 1)
            pe.wait_ge(s_thr, 1)

            def tile(n, b, free):
                if free is not None:
                    pe.wait_ge(s_copy, free)
                for w in range(PIECES):
                    for c in range(2):
                        wait_alone(pe, s_turn, n * (2 * PIECES) + (2 * w + c + 1))
                        for e in range(PACK):
                            for k in range(PB):
                                m = w * PCH + e * PB + k
                                for a in range(2):
                                    last = nc.tensor.matmul(acc[b][c][a][:, 0:FD], turned[:, w, c, k, :, e],
                                                            tables[:, c, m, a, 0:FD], start=(m == 0), stop=(m == CH - 1))
                    last.then_inc(s_mm, 1)

            for b in range(2):
                tile(b, b, None)
            with pe.Fori(1, TILES // 2) as v:
                for b in range(2):
                    tile(v * 2 + b, b, v * 2 + (b - 1))


def kernel(x, adj, L0_gnn_W1, L0_gnn_b1, L0_gnn_a1, L0_gnn_a2, L0_gnn_b2):
    import numpy as _np
    import concourse.bacc as _bacc
    from concourse import mybir as _mybir
    from concourse.bass_utils import run_bass_kernel_spmd as _run

    nc = _bacc.Bacc("TRN2", target_bir_lowering=False, num_devices=1, dynamic_dma_scratch_size=4096)
    given = {"x": x, "adj": adj, "w1": L0_gnn_W1, "b1": L0_gnn_b1, "a1": L0_gnn_a1, "a2": L0_gnn_a2, "b2": L0_gnn_b2}
    arrays, args = {}, []
    for name, value in given.items():
        a = _np.ascontiguousarray(value)
        if name == "b2":
            a = a.reshape(1)
        arrays[f"in_{name}"] = a
        args.append(nc.dram_tensor(f"in_{name}", a.shape, _mybir.dt.from_np(a.dtype), kind="ExternalInput").ap())
    out = nc.dram_tensor("out", given["x"].shape, F32, kind="ExternalOutput").ap()
    adjacency_attention(nc, *args, out)
    r = _run(nc, [arrays], core_ids=[0])
    return r.results[0]["out"]
```

```python
from contextlib import ExitStack

import concourse.bass as bass
from concourse import mybir

F32 = mybir.dt.float32
F16 = mybir.dt.float16
F8 = mybir.dt.float8e4
I32 = mybir.dt.int32
U32 = mybir.dt.uint32
ALU = mybir.AluOpType
ACT = mybir.ActivationFunctionType
AX_X = mybir.AxisListType.X
RMAX = bass.bass_isa.ReduceOp.max

P = 128
QUADS = 4
R = P // QUADS
ALPHA = 0.2
EPS = 1e-5
PLUS, MINUS = 0, 1
HIGH, LOW = 0, 1
LOW_SCALE = 4096.0
TABLE_SHIFT = 8.0 * 0.6931471805599453
ROUND = 12582912.0
MIXED, ONE_PLUS, ONE_MINUS = 0, 1, 2
MARGIN = 2.0 ** -20
CREDIT = {"s_last": 4, "s_tlast": 4, "s_mlast": 2, "s_mfirst": 1, "s_sum": 2, "s_half": 1,
          "s_lo": 4, "s_pick": 2}


def adjacency_attention(nc, x, adj, w1, b1, a1, a2, b2, out):
    N, F = x.shape
    QN = N // QUADS
    CH = QN // R
    FD = F + 1
    FE = F + 2
    KK = F // P
    PACK = 4
    PB = QN // (R * PACK)
    TILES = N // P
    PAIRS = TILES // 2
    GX = 8
    GROUPS = CH // GX
    RING = 4
    TB = 4
    HG = 2 * TB

    x_rows = x.rearrange("(g n) f -> g n f", g=QUADS)
    adj_rows = adj.rearrange("n (q j) -> (n q) j", q=QUADS)

    ctx = ExitStack()
    with ctx:
        def sb(name, shape, dt):
            return ctx.enter_context(nc.sbuf_tensor(name, shape, dt))

        def sem(name):
            return ctx.enter_context(nc.semaphore(name))

        tables = sb("tables", [P, 2, CH, 2, FE], F16)
        h32 = tables[:, PLUS, :, :, :].rearrange("p m a f -> p m (a f)").bitcast(F32)
        early = tables[:, MINUS, :, :, :].rearrange("p m a f -> p (m a f)").bitcast(F32)
        xs = early[:, 0:2 * GX * F].rearrange("p (u k f) -> p u k f", u=2, k=GX)
        hn = early[:, 4096:4096 + RING * F].rearrange("p (k f) -> p k f", k=RING)
        hnT = early[:, 5120:5120 + RING * F].rearrange("p (k a i) -> p k a i", k=RING, a=KK)
        w1_sb = early[:, 6144:6144 + KK * FE].rearrange("p (a f) -> p a f", a=KK)
        a_bc = early[:, 6660:6660 + 2 * F].rearrange("p (a f) -> p a f", a=2)
        b_bc = early[:, 7172:7172 + FE]
        junk = early[:, 7430:7430 + F]

        adj_ring = sb("adj_ring", [P, QUADS, QN], I32)
        sorting = adj_ring[:, :, :].rearrange("p g j -> p (g j)").bitcast(F32)
        is_lo = sorting[:, 0:2 * HG * P].rearrange("p (s k i) -> p s k i", s=2, k=HG)
        is_hi = sorting[:, 2048:2048 + 2 * HG * TILES].rearrange("p (s k t) -> p s k t", s=2, k=HG)
        picked = sorting[:, 3072:3072 + 4 * HG * TILES].rearrange("p (s k v t) -> p s k v t", s=2, k=HG, v=2)
        spread = sorting[:, 5120:5120 + QN].rearrange("p (m c) -> p m c", c=R)

        tau = sb("tau", [P, 2, QN], F32)
        work = sb("work", [P, 6 * 1024], F32)
        workb = work[:, :].bitcast(F8)
        masks = workb[:, 0:4 * QN].rearrange("p (g w e) -> p g w e", g=QUADS, e=PACK)
        turned = workb[:, 4 * QN:12 * QN].rearrange("p (s b i e) -> p s b i e", s=2, b=PB, e=PACK)
        scaled = work[:, 0:4 * TB * F].rearrange("p (s c k f) -> p s c k f", s=2, c=2, k=TB)
        ident = work[:, 4096:4096 + P]
        pick = work[:, 4224:4224 + QUADS * P].rearrange("p (g q r) -> p g q r", g=QUADS, q=QUADS)
        quad_ones = work[:, 4736:4736 + P]
        eye32 = work[:, 4864:4864 + R]
        all_ones = work[:, 4896:4896 + P]
        lower = work[:, 5024:5024 + P]
        count = work[:, 5152:5152 + P]
        row_no = work[:, 5280:5280 + CH]

        st = sb("st", [P, 2, CH], F32)
        late = sb("late", [P, 4 * FD + 6 * F], F32)
        parts = late[:, 0:4 * FD].rearrange("p (b c f) -> p b c f", b=2, c=2)
        xt = late[:, 4 * FD:4 * FD + 2 * F].rearrange("p (b f) -> p b f", b=2)
        ot = late[:, 4 * FD + 2 * F:4 * FD + 4 * F].rearrange("p (b f) -> p b f", b=2)
        ex = late[:, 4 * FD + 4 * F:4 * FD + 5 * F]
        pos = late[:, 4 * FD + 5 * F:4 * FD + 6 * F]
        taken = [0]

        def before(*dims):
            size = 1
            for d in dims:
                size *= d
            part = late[:, taken[0]:taken[0] + size]
            taken[0] += size
            axes = "abcd"[:len(dims)]
            if len(dims) == 1:
                return part
            return part.rearrange(f"p ({' '.join(axes)}) -> p {' '.join(axes)}", **dict(zip(axes[:-1], dims[:-1])))

        stats = before(2, GX, 6)
        mv = before(2, GX, 2)
        sd = before(2, GX)
        rstd = before(2, GX)
        shift = before(2, GX)
        hsum = before(F)
        grid = before(2, CH)
        grid2 = before(2, CH)
        kind = before(3, CH)
        total = before(3, CH)
        upto = before(3, CH)
        place = before(3, CH)
        zero = before(CH)
        step = before(2, CH)
        slot = before(4, CH)
        row_s = before(2, TILES)
        row_psi = before(TILES)
        tmp_t = before(TILES)
        hmean = sb("hmean", [P, F], F32)
        b2_bc = sb("b2_bc", [P, 1], F32)
        eps_col = sb("eps_col", [P, 1], F32)
        quad = sb("quad", [P, 1], F32)
        ends = sb("ends", [P, 2], F32)
        span = sb("span", [P, 2], F32)
        k0 = sb("k0", [P, 1], F32)
        k1 = sb("k1", [P, 1], F32)
        k2 = sb("k2", [P, 1], F32)
        ebias = sb("ebias", [P, 2], F32)
        full = sb("full", [P, 3], F32)
        full2 = sb("full2", [P, 3], F32)
        rest = sb("rest", [P, 3], F32)
        base = sb("base", [P, 1], F32)
        jump = sb("jump", [P, 3], F32)
        ends_i = sb("ends_i", [P, 2], I32)
        psi = sb("psi", [P, 2, QUADS, TILES], F32)
        psi_now = sb("psi_now", [P, 2, QUADS], F32)
        adj_idx = sb("adj_idx", [P, QUADS, TILES], U32)
        row_idx = sb("row_idx", [P, TILES], U32)
        adj_idx_now = sb("adj_idx_now", [P, 2, QUADS], U32)
        x_idx_now = sb("x_idx_now", [P, 2], U32)
        out_idx_now = sb("out_idx_now", [P, 2], U32)
        z = sb("z", [P, TILES], F32)
        gamma = sb("gamma", [P, TILES], F32)
        gamma_low = sb("gamma_low", [P, TILES], F32)
        fac = sb("fac", [P, 2, CH], F32)
        fac_low = sb("fac_low", [P, 2, CH], F32)
        flag = sb("flag", [P, 1], F32)
        den = sb("den", [P, 1], F32)
        rden = sb("rden", [P, 1], F32)

        acc = [[[ctx.enter_context(nc.psum_tensor(f"acc{b}{c}{a}", [P, 512], F32)) for a in range(2)]
                for c in range(2)] for b in range(2)]
        bank = [acc[b][c][a] for b in range(2) for c in range(2) for a in range(2)]
        ROWS, CUM, MEAN, PICK_ROW, PICK_PSI = 6, 7, 5, 4, 7

        s_const = sem("s_const")
        s_eye = sem("s_eye")
        s_x = [[sem(f"s_x{h}{k}") for k in range(GX)] for h in range(2)]
        s_norm = sem("s_norm")
        s_var = sem("s_var")
        s_sd = sem("s_sd")
        s_rs = sem("s_rs")
        s_tp = sem("s_tp")
        s_tc = sem("s_tc")
        s_hp = sem("s_hp")
        s_h = sem("s_h")
        s_w = sem("s_w")
        s_hs = sem("s_hs")
        s_mean = sem("s_mean")
        s_ends = sem("s_ends")
        s_span = sem("s_span")
        s_kind = sem("s_kind")
        s_cum = sem("s_cum")
        s_lists = sem("s_lists")
        s_spread = sem("s_spread")
        s_bc = sem("s_bc")
        s_tau = sem("s_tau")
        s_onehot = sem("s_onehot")
        s_pick = sem("s_pick")
        s_slot = sem("s_slot")
        s_quads = sem("s_quads")
        s_idx = sem("s_idx")
        s_gam = sem("s_gam")
        s_gl = sem("s_gl")
        s_eb = sem("s_eb")
        s_exp = sem("s_exp")
        s_fac = sem("s_fac")
        s_scx = sem("s_scx")
        s_scy = sem("s_scy")
        s_hi = sem("s_hi")
        s_lo = sem("s_lo")
        s_adj = [sem(f"s_adj{g}") for g in range(QUADS)]
        s_first = sem("s_first")
        s_last = sem("s_last")
        s_psi = sem("s_psi")
        s_tfirst = sem("s_tfirst")
        s_tlast = sem("s_tlast")
        s_mfirst = sem("s_mfirst")
        s_mlast = sem("s_mlast")
        s_ic = sem("s_ic")
        s_xt = [sem(f"s_xt{b}") for b in range(2)]
        s_copy = sem("s_copy")
        s_mix = sem("s_mix")
        s_sum = sem("s_sum")
        s_tail = sem("s_tail")
        s_num = sem("s_num")
        s_elu = sem("s_elu")
        s_half = sem("s_half")
        s_ot = sem("s_ot")
        s_out = [sem(f"s_out{b}") for b in range(2)]
        s_passed = sem("s_passed")
        s_dve = sem("s_dve")

        def wait_alone(eng, semaphore, value):
            eng.wait_ge(semaphore, value)
            eng.sem_inc(s_passed, 1)

        def list_ends(eng):
            eng.wait_ge(s_lists, 1)
            return [eng.value_load(ends_i[0:1, k:k + 1], min_val=0, max_val=TILES) for k in range(2)]

        def by_kind(eng, T, lists, make):
            with eng.If(T < lists[0]):
                make(ONE_PLUS)
            with eng.Else():
                with eng.If(T < lists[1]):
                    make(ONE_MINUS)
                with eng.Else():
                    make(MIXED)

        block = ctx.enter_context(nc.Block())

        @block.sync
        def _(sp):
            for k in range(GX):
                sp.dma_start(xs[:, 0, k, :], x_rows[:, k * R:(k + 1) * R, :]).then_inc(s_x[0][k], 16)
            sp.dma_start(w1_sb[:, :, 0:F], w1.rearrange("(a k) f -> k a f", a=KK)).then_inc(s_const, 16)
            sp.dma_start(a_bc[:, 0, :], a1.rearrange("(o f) -> o f", o=1).broadcast_to((P, F))).then_inc(s_const, 16)
            sp.dma_start(a_bc[:, 1, :], a2.rearrange("(o f) -> o f", o=1).broadcast_to((P, F))).then_inc(s_const, 16)
            sp.dma_start(b_bc[:, 0:F], b1.rearrange("(o f) -> o f", o=1).broadcast_to((P, F))).then_inc(s_const, 16)
            sp.dma_start(b2_bc[:, :], b2.rearrange("(o f) -> o f", o=1).broadcast_to((P, 1))).then_inc(s_const, 16)

            def load_group(u, half_, m0, after):
                for k in range(GX):
                    if after is not None:
                        sp.wait_ge(s_norm, after + k)
                    sp.dma_start(xs[:, half_, k, :], x_rows[:, bass.ds(m0 + k * R, R), :]).then_inc(s_x[half_][k], 16)

            load_group(1, 1, GX * R, None)
            with sp.Fori(1, GROUPS // 2) as v:
                for o in range(2):
                    load_group(None, o, v * (2 * GX * R) + o * GX * R, v * (2 * GX) + ((o - 2) * GX + 1))

        @block.gpsimd
        def _(pool):
            step = [0]

            def done(ins):
                step[0] += 1
                ins.then_inc(s_eye, 1)
                pool.wait_ge(s_eye, step[0])

            done(nc.gpsimd.memset(work[:, 4096:4896], 0.0))
            done(nc.gpsimd.affine_select(out=ident, in_=ident, compare_op=ALU.not_equal, fill=1.0, base=0,
                                         pattern=[[-1, P]], channel_multiplier=1))
            done(nc.gpsimd.memset(work[:, 4896:5152], 1.0))
            for g in range(QUADS):
                done(nc.gpsimd.affine_select(out=pick[:, g, :, :], in_=pick[:, g, :, :], compare_op=ALU.not_equal,
                                             fill=1.0, base=-R * g, pattern=[[0, QUADS], [-1, R]],
                                             channel_multiplier=1))
                done(nc.gpsimd.affine_select(out=eye32, in_=eye32, compare_op=ALU.not_equal, fill=1.0, base=-R * g,
                                             pattern=[[-1, R]], channel_multiplier=1))
                done(nc.gpsimd.memset(quad_ones[R * g:R * g + R, R * g:R * g + R], 1.0))
                done(nc.gpsimd.memset(quad[R * g:R * g + R, :], float(g)))
                done(nc.gpsimd.iota(row_no[R * g:R * g + R, :], pattern=[[R, CH]], base=QN * g, channel_multiplier=1,
                                    allow_small_or_imprecise_dtypes=True))
            done(nc.gpsimd.affine_select(out=lower, in_=lower, compare_op=ALU.is_gt, fill=0.0, base=0,
                                         pattern=[[1, P]], channel_multiplier=-1))
            done(nc.gpsimd.iota(count, pattern=[[1, P]], base=0, channel_multiplier=0,
                                allow_small_or_imprecise_dtypes=True))
            done(nc.gpsimd.memset(hsum, 0.0))
            pool.wait_ge(s_h, 1)
            nc.gpsimd.tensor_tensor(hsum, hsum, h32[:, 0, 0:F], ALU.add).then_inc(s_hs, 1)
            with pool.Fori(1, CH) as m:
                pool.wait_ge(s_h, m + 1)
                pool.wait_ge(s_hs, m)
                nc.gpsimd.tensor_tensor(hsum, hsum, h32[:, m, 0:F], ALU.add).then_inc(s_hs, 1)
            pool.wait_ge(s_ends, 1)
            nc.gpsimd.partition_all_reduce(span[:, :], ends[:, :], P, RMAX).then_inc(s_span, 1)

            pool.wait_ge(s_fac, 1)
            with pool.Fori(0, CH // HG) as v:
                for o in range(2):
                    pool.wait_ge(s_lo, v * 4 + (2 * o - 2 + CREDIT["s_lo"]))
                    nc.gpsimd.tensor_tensor(
                        scaled[:, o, MINUS, :, :], h32[:, bass.ds(v * HG + o * TB, TB), 0:F],
                        fac_low[:, MINUS, bass.ds(v * HG + o * TB, TB)].rearrange("p (k i) -> p k i", i=1)
                        .broadcast_to((P, TB, F)), ALU.mult).then_inc(s_scy, 1)

            pool.wait_ge(s_idx, 1)

            def set_out(T, b, x_too, out_too, G):
                if not isinstance(G, int) or G > 1:
                    wait_alone(pool, s_xt[b], G * 16 - 16)
                if not isinstance(G, int) or G + b > 2:
                    wait_alone(pool, s_out[1 - b], G * 16 + (b * 16 - 32))
                last = nc.gpsimd.tensor_copy(adj_idx_now[:, b, :], adj_idx[:, :, bass.ds(T, 1)].rearrange("p g o -> p (g o)"))
                last.then_inc(s_ic, 1)
                if x_too:
                    nc.gpsimd.tensor_copy(x_idx_now[:, b:b + 1], row_idx[:, bass.ds(T - 2, 1)]).then_inc(s_ic, 1)
                else:
                    pool.sem_inc(s_ic, 1)
                if out_too:
                    nc.gpsimd.tensor_copy(out_idx_now[:, 1 - b:2 - b], row_idx[:, bass.ds(T - 3, 1)]).then_inc(s_ic, 1)
                else:
                    pool.sem_inc(s_ic, 1)
                wait_alone(pool, s_ic, T * 3 + 3)

            def load_adj(T, b):
                for g in range(QUADS):
                    wait_alone(pool, s_last, T * 4 + (g + 1))
                    nc.gpsimd.indirect_dma_start(adj_ring[:, g, :], None, adj_rows,
                                                 bass.IndirectOffsetOnAxis(ap=adj_idx_now[:, b, g:g + 1], axis=0))\
                      .then_inc(s_adj[g], 16)

            def load_x(b):
                nc.gpsimd.indirect_dma_start(xt[:, b, :], None, x,
                                             bass.IndirectOffsetOnAxis(ap=x_idx_now[:, b:b + 1], axis=0))\
                  .then_inc(s_xt[b], 16)

            def store(S, b):
                wait_alone(pool, s_ot, S + 1)
                nc.gpsimd.indirect_dma_start(out, bass.IndirectOffsetOnAxis(ap=out_idx_now[:, b:b + 1], axis=0),
                                             ot[:, b, :], None)\
                  .then_inc(s_out[b], 16)

            def pair(G, with_x, with_out):
                for b in range(2):
                    T = G * 2 + b
                    set_out(T, b, with_x, with_out[b], G)
                    load_adj(T, b)
                    if with_x:
                        load_x(b)
                    if with_out[b]:
                        store(T - 3, 1 - b)

            pair(0, False, (False, False))
            pair(1, True, (False, True))
            pair(2, True, (True, True))
            with pool.Fori(3, PAIRS) as G:
                pair(G, True, (True, True))
            for b in range(2):
                pool.wait_ge(s_xt[b], (PAIRS - 1) * 16)
                pool.wait_ge(s_out[1 - b], (PAIRS - 2 + b) * 16)
                nc.gpsimd.tensor_copy(x_idx_now[:, b:b + 1], row_idx[:, TILES - 2 + b:TILES - 1 + b]).then_inc(s_ic, 1)
                nc.gpsimd.tensor_copy(out_idx_now[:, 1 - b:2 - b], row_idx[:, TILES - 3 + b:TILES - 2 + b]).then_inc(s_ic, 1)
                pool.wait_ge(s_ic, TILES * 3 + 2 * b + 2)
                load_x(b)
                store(TILES - 3 + b, 1 - b)
            pool.wait_ge(s_out[1], (PAIRS - 1) * 16)
            nc.gpsimd.tensor_copy(out_idx_now[:, 1:2], row_idx[:, TILES - 1:TILES]).then_inc(s_ic, 1)
            pool.wait_ge(s_ic, TILES * 3 + 5)
            store(TILES - 1, 1)
            for b in range(2):
                pool.wait_ge(s_out[b], PAIRS * 16)

        @block.scalar
        def _(act):
            act.wait_ge(s_dve, 1)

            def deviation(h):
                nc.scalar.activation(sd[:, h, :], mv[:, h, :, 1], ACT.Sqrt, bias=eps_col[:, :]).then_inc(s_sd, 1)

            def copy_turned(m, c):
                act.wait_ge(s_tp, m + (c + 1))
                if not isinstance(m, int) or m + c >= RING:
                    act.wait_ge(s_hp, m + (c + 1 - RING))
                nc.scalar.activation(hnT[:, c % RING, :, :], bank[c % RING][:, 0:F].rearrange("p (a i) -> p a i", a=KK),
                                     ACT.Copy).then_inc(s_tc, 1)

            def group(m, h, nth, use, final):
                act.wait_ge(s_rs, nth)
                for k in range(GX):
                    act.wait_ge(s_x[h][k], use * 16)
                    if not isinstance(m, int) or m + k >= RING:
                        act.wait_ge(s_tp, m + (k + 1 - RING))
                    nc.scalar.activation(hn[:, k % RING, :], xs[:, h, k, :], ACT.Relu, scale=rstd[:, h, k:k + 1],
                                         bias=shift[:, h, k:k + 1]).then_inc(s_norm, 1)
                    if k >= 1:
                        copy_turned(m, k - 1)
                    if k == 3 and not final:
                        act.wait_ge(s_var, nth + 1)
                        deviation(1 - h)
                copy_turned(m, GX - 1)

            act.wait_ge(s_var, 1)
            deviation(0)
            group(0, 0, 1, 1, False)
            group(GX, 1, 2, 1, False)
            with act.Fori(1, GROUPS // 2 - 1) as v:
                for o in range(2):
                    group(v * (2 * GX) + o * GX, o, v * 2 + (o + 1), v + 1, False)
            group(CH - 2 * GX, 0, GROUPS - 1, GROUPS // 2, False)
            group(CH - GX, 1, GROUPS, GROUPS // 2, True)

            act.wait_ge(s_eb, 1)
            nc.scalar.activation(fac[:, PLUS, :], st[:, 1, :], ACT.Exp, bias=ebias[:, 0:1])
            nc.scalar.activation(fac[:, MINUS, :], st[:, 1, :], ACT.Exp, bias=ebias[:, 1:2], scale=ALPHA).then_inc(s_exp, 1)

            act.wait_ge(s_bc, 1)
            for q in range(QN // 512):
                nc.scalar.activation(tau[:, PLUS, 512 * q:512 * q + 512], bank[q][:, :], ACT.Copy)
                last = nc.scalar.activation(tau[:, MINUS, 512 * q:512 * q + 512], bank[q][:, :], ACT.Identity, scale=-1.0,
                                            bias=all_ones[:, 0:1])
            last.then_inc(s_tau, 1)

            act.wait_ge(s_fac, 1)
            with act.Fori(0, CH // HG) as v:
                for o in range(2):
                    act.wait_ge(s_lo, v * 4 + (2 * o - 2 + CREDIT["s_lo"]))
                    for k in range(TB):
                        last = nc.scalar.activation(scaled[:, o, PLUS, k, :], h32[:, v * HG + (o * TB + k), 0:F], ACT.Copy,
                                                    scale=fac_low[:, PLUS, bass.ds(v * HG + (o * TB + k), 1)])
                    last.then_inc(s_scx, 1)
                    act.wait_ge(s_scy, v * 2 + (o + 1))
                    nc.scalar.activation(tables[:, MINUS, bass.ds(v * HG + o * TB, TB), HIGH, 0:F], scaled[:, o, MINUS, :, :],
                                         ACT.Copy, scale=1.0 / LOW_SCALE).then_inc(s_hi, 1)
                    act.wait_ge(s_scx, v * 2 + (o + 1))
                    nc.scalar.activation(tables[:, PLUS, bass.ds(v * HG + o * TB, TB), HIGH, 0:F], scaled[:, o, PLUS, :, :],
                                         ACT.Copy, scale=1.0 / LOW_SCALE).then_inc(s_hi, 1)
            act.wait_ge(s_lo, 2 * (CH // TB) + CREDIT["s_lo"])
            for c in range(2):
                last = nc.scalar.activation(tables[:, c, :, HIGH, F], fac[:, c, :], ACT.Copy)
            last.then_inc(s_hi, 1)
            act.wait_ge(s_slot, 2)
            nc.scalar.activation(gamma[:, :], z[:, :], ACT.Exp, scale=-(1.0 - ALPHA)).then_inc(s_gam, 1)

            lists = list_ends(act)
            act.wait_ge(s_gam, 1)

            def tile(T, b, what):
                act.wait_ge(s_mlast, T + (1 + CREDIT["s_mlast"]))
                act.wait_ge(s_sum, T + (CREDIT["s_sum"] - 1))
                first = nc.scalar.activation(parts[:, b, 0, :], acc[b][0][HIGH][:, 0:FD], ACT.Copy)
                if what == MIXED:
                    nc.scalar.activation(parts[:, b, 1, :], acc[b][1][HIGH][:, 0:FD], ACT.Copy,
                                         scale=gamma[:, bass.ds(T, 1)]).then_inc(s_copy, 1)
                else:
                    first.then_inc(s_copy, 1)
                act.wait_ge(s_num, T + 1)
                act.wait_ge(s_half, T + CREDIT["s_half"])
                nc.scalar.activation(ex, parts[:, b, 0, 0:F], ACT.Exp, scale=rden[:, :])
                nc.scalar.activation(pos, parts[:, b, 0, 0:F], ACT.Relu, scale=rden[:, :]).then_inc(s_elu, 1)

            with act.Fori(0, PAIRS) as G:
                for b in range(2):
                    by_kind(act, G * 2 + b, lists, lambda what: tile(G * 2 + b, b, what))

        @block.vector
        def _(dve):
            chain = [0]

            def link(ins):
                chain[0] += 1
                ins.then_inc(s_dve, 1)
                dve.wait_ge(s_dve, chain[0])

            for name, semaphore in (("s_last", s_last), ("s_tlast", s_tlast), ("s_sum", s_sum),
                                    ("s_half", s_half), ("s_lo", s_lo)):
                dve.sem_inc(semaphore, CREDIT[name])
            link(nc.vector.memset(eps_col[:, :], EPS))
            link(nc.vector.memset(zero[:, :], 0.0))

            def statistics(h, use, n0):
                for k in range(GX):
                    dve.wait_ge(s_x[h][k], use * 16)
                    nc.vector.bn_stats(stats[:, h, k, :], xs[:, h, k, :]).then_inc(s_dve, 1)
                wait_alone(dve, s_dve, n0 + GX)
                for k in range(GX):
                    last = nc.vector.bn_aggr(mv[:, h, k, :], stats[:, h, k, :])
                    last.then_inc(s_var if k == GX - 1 else s_dve, 1)

            def scale_and_shift(h, nth, n0):
                dve.wait_ge(s_sd, nth)
                nc.vector.reciprocal(rstd[:, h, :], sd[:, h, :]).then_inc(s_dve, 1)
                dve.wait_ge(s_dve, n0 + 2 * GX)
                nc.vector.scalar_tensor_tensor(out=shift[:, h, :], in0=mv[:, h, :, 0], scalar=-1.0, in1=rstd[:, h, :],
                                               op0=ALU.mult, op1=ALU.mult).then_inc(s_rs, 1)

            def store_h(m, k):
                dve.wait_ge(s_hp, m + (k + 1))
                nc.vector.tensor_tensor(h32[:, m + k, 0:FE], bank[RING + k % RING][:, 0:FE], b_bc, ALU.add).then_inc(s_h, 1)

            def group(m, h, nth, use, n0, final):
                if not final:
                    statistics(1 - h, use + h, n0 + 2 * GX)
                for k in range(GX // 2):
                    store_h(m, k)
                if not final:
                    scale_and_shift(1 - h, nth + 1, n0 + 2 * GX)
                for k in range(GX // 2, GX):
                    store_h(m, k)

            C0 = chain[0]
            statistics(0, 1, C0)
            scale_and_shift(0, 1, C0)
            chain[0] += 2 * GX
            C1 = chain[0]
            dve.wait_ge(s_const, 80)
            for c in range(2):
                for a in range(KK):
                    link(nc.vector.scalar_tensor_tensor(out=junk, in0=w1_sb[:, a, 0:F], scalar=1.0, in1=a_bc[:, c, :],
                                                        op0=ALU.mult, op1=ALU.mult,
                                                        accum_out=w1_sb[:, a, F + c:F + c + 1]))
                link(nc.vector.scalar_tensor_tensor(out=junk, in0=b_bc[:, 0:F], scalar=1.0, in1=a_bc[:, c, :],
                                                    op0=ALU.mult, op1=ALU.mult, accum_out=b_bc[:, F + c:F + c + 1]))
            nc.vector.tensor_tensor(b_bc[:, F:F + 1], b_bc[:, F:F + 1], b2_bc[:, :], ALU.add).then_inc(s_w, 1)
            dve.wait_ge(s_w, 1)
            D0 = chain[0] - 2 * GX
            group(0, 0, 1, 1, D0, False)
            group(GX, 1, 2, 1, D0 + 2 * GX, False)
            with dve.Fori(1, GROUPS // 2 - 1) as v:
                for o in range(2):
                    group(v * (2 * GX) + o * GX, o, v * 2 + (o + 1), v + 1, v * (4 * GX) + (D0 + o * 2 * GX), False)
            group(CH - 2 * GX, 0, GROUPS - 1, GROUPS // 2, D0 + 2 * GX * (GROUPS - 2), False)
            group(CH - GX, 1, GROUPS, GROUPS // 2, None, True)
            chain[0] = D0 + 2 * GX * GROUPS

            dve.wait_ge(s_h, CH)
            link(nc.vector.tensor_copy(st[:, :, :], h32[:, :, F:FE].rearrange("p m c -> p c m")))
            link(nc.vector.tensor_reduce(ends[:, 0:1], st[:, 1, :], AX_X, ALU.max))
            link(nc.vector.tensor_reduce(ends[:, 1:2], st[:, 1, :], AX_X, ALU.min))
            nc.vector.tensor_scalar(ends[:, 1:2], ends[:, 1:2], -1.0, None, ALU.mult).then_inc(s_ends, 1)
            dve.wait_ge(s_span, 1)
            link(nc.vector.tensor_scalar(ebias[:, 0:1], span[:, 0:1], -1.0, TABLE_SHIFT, ALU.mult, ALU.add))
            nc.vector.tensor_scalar(ebias[:, 1:2], span[:, 0:1], -ALPHA, TABLE_SHIFT, ALU.mult, ALU.add).then_inc(s_eb, 1)
            link(nc.vector.tensor_tensor(k0[:, :], span[:, 0:1], span[:, 1:2], ALU.add))
            link(nc.vector.tensor_scalar(k1[:, :], k0[:, :], 2.0, 1e-30, ALU.mult, ALU.max))
            link(nc.vector.reciprocal(k2[:, :], k1[:, :]))

            def threshold(dst, src, tmp):
                link(nc.vector.tensor_scalar(dst, src, span[:, 0:1], k2[:, :], ALU.add, ALU.mult))
                link(nc.vector.tensor_scalar(tmp, dst, -0.125, 0.625, ALU.max, ALU.min))
                link(nc.vector.tensor_scalar(dst, tmp, 1.25, -1.0, ALU.add, ALU.add))

            link(nc.vector.tensor_scalar(grid2[:, 1, :], st[:, 1, :], -1.0, None, ALU.mult))
            threshold(grid[:, 0, :], st[:, 0, :], grid2[:, 0, :])
            link(nc.vector.tensor_scalar(kind[:, ONE_PLUS, :], grid[:, 0, :], 0.75 + MARGIN, None, ALU.is_gt))
            link(nc.vector.tensor_scalar(kind[:, ONE_MINUS, :], grid[:, 0, :], 0.25 - MARGIN, None, ALU.is_lt))
            link(nc.vector.tensor_tensor(grid2[:, 0, :], kind[:, ONE_PLUS, :], kind[:, ONE_MINUS, :], ALU.add))
            nc.vector.tensor_scalar(kind[:, MIXED, :], grid2[:, 0, :], -1.0, 1.0, ALU.mult, ALU.add).then_inc(s_kind, 1)
            dve.wait_ge(s_exp, 1)
            nc.vector.tensor_scalar(fac_low[:, :, :], fac[:, :, :], LOW_SCALE, None, ALU.mult).then_inc(s_fac, 1)
            threshold(grid[:, 1, :], grid2[:, 1, :], grid2[:, 0, :])
            nc.vector.tensor_tensor(spread[:, :, :], grid[:, 1, :].rearrange("p (m o) -> p m o", o=1).broadcast_to((P, CH, R)),
                                    eye32.rearrange("p (o c) -> p o c", o=1).broadcast_to((P, CH, R)), ALU.mult)\
              .then_inc(s_spread, 1)

            dve.wait_ge(s_cum, 1)
            link(nc.vector.tensor_copy(total[:, :, :], bank[CUM][:, 3 * CH:6 * CH].rearrange("p (k m) -> p k m", k=3)))
            for k in range(3):
                link(nc.vector.tensor_tensor_scan(upto[:, k, :], total[:, k, :], zero[:, :], 0.0, ALU.add, ALU.add))
            link(nc.vector.tensor_scalar(full2[:, :], upto[:, :, CH - 1], 1.0 / P, -0.498, ALU.mult, ALU.add))
            link(nc.vector.tensor_scalar(full2[:, :], full2[:, :], ROUND, -ROUND, ALU.add, ALU.add))
            link(nc.vector.tensor_copy(ends_i[:, 0:1], full2[:, ONE_PLUS:ONE_PLUS + 1]))
            nc.vector.tensor_tensor(ends_i[:, 1:2], full2[:, ONE_PLUS:ONE_PLUS + 1], full2[:, ONE_MINUS:ONE_MINUS + 1],
                                    ALU.add).then_inc(s_lists, 1)
            link(nc.vector.tensor_scalar(full[:, :], full2[:, :], float(P), None, ALU.mult))
            link(nc.vector.tensor_tensor(rest[:, :], upto[:, :, CH - 1], full[:, :], ALU.subtract))
            link(nc.vector.tensor_tensor(base[:, :], full[:, ONE_PLUS:ONE_PLUS + 1],
                                         full[:, ONE_MINUS:ONE_MINUS + 1], ALU.add))
            link(nc.vector.tensor_tensor(jump[:, ONE_PLUS:ONE_PLUS + 1], full[:, ONE_MINUS:ONE_MINUS + 1],
                                         upto[:, MIXED, CH - 1:CH], ALU.add))
            link(nc.vector.tensor_tensor(jump[:, ONE_MINUS:ONE_MINUS + 1], rest[:, ONE_PLUS:ONE_PLUS + 1],
                                         upto[:, MIXED, CH - 1:CH], ALU.add))
            link(nc.vector.tensor_tensor(place[:, :, :], upto[:, :, :], total[:, :, :], ALU.subtract))
            link(nc.vector.tensor_tensor(upto[:, :, :], place[:, :, :],
                                         bank[CUM][:, 0:3 * CH].rearrange("p (k m) -> p k m", k=3), ALU.add))
            for k in (ONE_PLUS, ONE_MINUS):
                link(nc.vector.tensor_scalar(step[:, k - 1, :], upto[:, k, :], full[:, k:k + 1], jump[:, k:k + 1],
                                             ALU.is_ge, ALU.mult))
            link(nc.vector.tensor_tensor(place[:, ONE_PLUS, :], upto[:, ONE_PLUS, :], step[:, 0, :], ALU.add))
            link(nc.vector.scalar_tensor_tensor(out=place[:, ONE_MINUS, :], in0=upto[:, ONE_MINUS, :],
                                                scalar=full[:, ONE_PLUS:ONE_PLUS + 1], in1=step[:, 1, :],
                                                op0=ALU.add, op1=ALU.add))
            link(nc.vector.tensor_scalar(place[:, MIXED, :], upto[:, MIXED, :], base[:, :], None, ALU.add))
            link(nc.vector.tensor_tensor(upto[:, :, :], place[:, :, :], kind[:, :, :], ALU.mult))
            link(nc.vector.tensor_tensor(slot[:, 0, :], upto[:, 0, :], upto[:, 1, :], ALU.add))
            link(nc.vector.tensor_tensor(slot[:, 1, :], slot[:, 0, :], upto[:, 2, :], ALU.add))
            link(nc.vector.tensor_scalar(slot[:, 0, :], slot[:, 1, :], 1.0 / P, -0.498, ALU.mult, ALU.add))
            link(nc.vector.tensor_scalar(slot[:, 2, :], slot[:, 0, :], ROUND, -ROUND, ALU.add, ALU.add))
            link(nc.vector.scalar_tensor_tensor(out=slot[:, 3, :], in0=slot[:, 2, :], scalar=-float(P), in1=slot[:, 1, :],
                                                op0=ALU.mult, op1=ALU.add))

            dve.wait_ge(s_mean, 1)
            link(nc.vector.tensor_scalar(hmean[:, :], bank[MEAN][:, 0:F], 1.0 / N, None, ALU.mult))

            E0 = chain[0]

            def rows_to_slots(v, o, j):
                m0 = v * (2 * HG) + o * HG
                wait_alone(dve, s_pick, j + (CREDIT["s_pick"] - 1))
                nc.vector.tensor_tensor(
                    is_lo[:, o, :, :], slot[:, 3, bass.ds(m0, HG)].rearrange("p (k i) -> p k i", i=1).broadcast_to((P, HG, P)),
                    count.rearrange("p (k i) -> p k i", k=1).broadcast_to((P, HG, P)), ALU.is_equal)
                nc.vector.tensor_tensor(
                    is_hi[:, o, :, :], slot[:, 2, bass.ds(m0, HG)].rearrange("p (k i) -> p k i", i=1).broadcast_to((P, HG, TILES)),
                    count[:, 0:TILES].rearrange("p (k i) -> p k i", k=1).broadcast_to((P, HG, TILES)), ALU.is_equal)\
                  .then_inc(s_dve, 1)
                dve.wait_ge(s_dve, j + (E0 + 1))
                nc.vector.tensor_tensor(
                    picked[:, o, :, 0, :], is_hi[:, o, :, :],
                    row_no[:, bass.ds(m0, HG)].rearrange("p (k i) -> p k i", i=1).broadcast_to((P, HG, TILES)), ALU.mult)
                nc.vector.tensor_tensor(
                    picked[:, o, :, 1, :], is_hi[:, o, :, :],
                    st[:, 0, bass.ds(m0, HG)].rearrange("p (k i) -> p k i", i=1).broadcast_to((P, HG, TILES)), ALU.mult)\
                  .then_inc(s_onehot, 1)

            def table_low(m0, o, j):
                for c, order in ((MINUS, 1), (PLUS, 2)):
                    dve.wait_ge(s_hi, j * 2 + order)
                    nc.vector.scalar_tensor_tensor(out=tables[:, c, bass.ds(m0, TB), LOW, 0:F],
                                                   in0=tables[:, c, bass.ds(m0, TB), HIGH, 0:F], scalar=-LOW_SCALE,
                                                   in1=scaled[:, o, c, :, :], op0=ALU.mult, op1=ALU.add).then_inc(s_lo, 1)

            with dve.Fori(0, CH // (2 * HG)) as v:
                for o in range(2):
                    rows_to_slots(v, o, v * 2 + o)
                    for p in range(2):
                        table_low(v * (2 * HG) + (o * HG + p * TB), p, v * 4 + (2 * o + p))
            chain[0] = E0 + CH // HG

            dve.wait_ge(s_pick, CH // HG + CREDIT["s_pick"])
            nc.vector.tensor_copy(row_s[:, :, :], bank[ROWS][:, 0:2 * TILES].rearrange("p (v t) -> p v t", v=2))\
              .then_inc(s_slot, 1)
            dve.wait_ge(s_slot, 1)
            nc.vector.tensor_copy(row_idx[:, :], row_s[:, 0, :])
            dve.wait_ge(s_quads, 1)
            nc.vector.tensor_scalar(adj_idx[:, :, :], bank[PICK_ROW][:, 0:QUADS * TILES].rearrange("p (g t) -> p g t", g=QUADS),
                                    float(QUADS), quad[:, :], ALU.mult, ALU.add).then_inc(s_idx, 1)
            threshold(row_psi[:, :], row_s[:, 1, :], tmp_t[:, :])
            nc.vector.tensor_scalar(z[:, :], row_s[:, 1, :], span[:, 0:1], 0.0, ALU.add, ALU.max).then_inc(s_slot, 1)
            dve.wait_ge(s_quads, 2)
            psi_q = bank[PICK_PSI][:, 0:QUADS * TILES].rearrange("p (g t) -> p g t", g=QUADS)
            link(nc.vector.tensor_scalar(psi[:, PLUS, :, :], psi_q, 1.0, None, ALU.mult))
            link(nc.vector.tensor_scalar(psi[:, MINUS, :, :], psi_q, -1.0, 1.0, ALU.mult, ALU.add))
            dve.wait_ge(s_hi, 2 * (CH // TB) + 1)
            for c in range(2):
                last = nc.vector.scalar_tensor_tensor(out=tables[:, c, :, LOW, F], in0=tables[:, c, :, HIGH, F],
                                                      scalar=-LOW_SCALE, in1=fac_low[:, c, :], op0=ALU.mult, op1=ALU.add)
            last.then_inc(s_lo, 1)
            dve.wait_ge(s_gam, 1)
            nc.vector.tensor_scalar(gamma_low[:, :], gamma[:, :], 1.0 / LOW_SCALE, None, ALU.mult).then_inc(s_gl, 1)
            dve.wait_ge(s_gl, 1)

            lists = list_ends(dve)
            dve.wait_ge(s_tau, 1)

            def make_masks(T, g, what, c):
                dst = masks[:, g, :, :].rearrange("p w e -> p e w")
                src = adj_ring[:, g, :].rearrange("p (e w) -> p e w", e=PACK)
                if c == PLUS or what != MIXED:
                    wait_alone(dve, s_adj[g], T * 16 + 16)
                    wait_alone(dve, s_tlast, T * 4 + (g + 1))
                else:
                    wait_alone(dve, s_tfirst, T * 4 + (g + 1))
                if what == MIXED:
                    nc.vector.scalar_tensor_tensor(out=dst, in0=src, scalar=psi_now[:, c, g:g + 1],
                                                   in1=tau[:, c, :].rearrange("p (e w) -> p e w", e=PACK), op0=ALU.min,
                                                   op1=ALU.is_gt if c == PLUS else ALU.is_ge, saturate=False)\
                      .then_inc(s_first if c == PLUS else s_last, 1)
                else:
                    nc.vector.tensor_scalar(dst, src, 0, None, ALU.is_gt, saturate=False).then_inc(s_last, 1)

            def turn(T, b, g, what, c):
                early_class = what == MIXED and c == PLUS
                if g == 0:
                    if early_class:
                        with dve.If(lists[1] < T):
                            wait_alone(dve, s_mfirst, T + CREDIT["s_mfirst"])
                        with dve.Else():
                            wait_alone(dve, s_mlast, T + CREDIT["s_mlast"])
                    elif what == MIXED:
                        dve.wait_ge(s_mlast, T + CREDIT["s_mlast"])
                    else:
                        dve.wait_ge(s_mlast, T + (CREDIT["s_mlast"] - 1))
                if early_class:
                    dve.wait_ge(s_first, T * 4 + (g + 1))
                else:
                    dve.wait_ge(s_last, T * 4 + (g + 1 + CREDIT["s_last"]))
                where = c if what == MIXED else b
                nc.vector.transpose(
                    turned[:, where, :, R * g:R * g + R, :].rearrange("p b r e -> p b (r e)").bitcast(U32),
                    masks[:, g, :, :].rearrange("p (b c) e -> p b (c e)", b=PB).bitcast(U32))\
                  .then_inc(s_tfirst if early_class else s_tlast, 1)

            def tile_sum(S, b, what):
                dve.wait_ge(s_copy, S + 1)
                if what == MIXED:
                    nc.vector.scalar_tensor_tensor(out=parts[:, b, 0, :], in0=acc[b][0][LOW][:, 0:FD], scalar=1.0 / LOW_SCALE,
                                                   in1=parts[:, b, 0, :], op0=ALU.mult, op1=ALU.add).then_inc(s_mix, 1)
                    nc.vector.scalar_tensor_tensor(out=parts[:, b, 1, :], in0=acc[b][1][LOW][:, 0:FD],
                                                   scalar=gamma_low[:, bass.ds(S, 1)], in1=parts[:, b, 1, :],
                                                   op0=ALU.mult, op1=ALU.add).then_inc(s_mix, 1)
                    dve.wait_ge(s_mix, S * 2 + 2)
                    nc.vector.tensor_tensor(parts[:, b, 0, :], parts[:, b, 0, :], parts[:, b, 1, :], ALU.add).then_inc(s_sum, 1)
                else:
                    dve.sem_inc(s_mix, 2)
                    nc.vector.scalar_tensor_tensor(out=parts[:, b, 0, :], in0=acc[b][0][LOW][:, 0:FD], scalar=1.0 / LOW_SCALE,
                                                   in1=parts[:, b, 0, :], op0=ALU.mult, op1=ALU.add).then_inc(s_sum, 1)

            def numerator(S, b):
                dve.wait_ge(s_sum, S + (1 + CREDIT["s_sum"]))
                nc.vector.tensor_scalar(flag[:, :], parts[:, b, 0, F:FD], 0.0, None, ALU.is_equal).then_inc(s_tail, 1)
                dve.wait_ge(s_tail, S * 3 + 1)
                nc.vector.tensor_tensor(den[:, :], parts[:, b, 0, F:FD], flag[:, :], ALU.add).then_inc(s_tail, 1)
                dve.wait_ge(s_tail, S * 3 + 2)
                nc.vector.reciprocal(rden[:, :], den[:, :]).then_inc(s_tail, 1)
                nc.vector.scalar_tensor_tensor(out=parts[:, b, 0, 0:F], in0=hmean[:, :], scalar=flag[:, :],
                                               in1=parts[:, b, 0, 0:F], op0=ALU.mult, op1=ALU.add).then_inc(s_num, 1)

            def result(S, b, nth):
                dve.wait_ge(s_elu, S + 1)
                if not isinstance(nth, int) or nth > 1:
                    dve.wait_ge(s_out[b], nth * 16 - 16)
                nc.vector.scalar_tensor_tensor(out=ot[:, b, :], in0=ex, scalar=1.0, in1=pos,
                                               op0=ALU.min, op1=ALU.add).then_inc(s_half, 1)
                dve.wait_ge(s_half, S + (1 + CREDIT["s_half"]))
                dve.wait_ge(s_xt[b], nth * 16)
                nc.vector.scalar_tensor_tensor(out=ot[:, b, :], in0=ot[:, b, :], scalar=-1.0, in1=xt[:, b, :],
                                               op0=ALU.add, op1=ALU.add).then_inc(s_ot, 1)

            def tile(T, b, nth, what):
                first = isinstance(nth, int) and nth == 0

                def sum_before():
                    if not first and what == MIXED:
                        with dve.If(T < lists[1] + 2):
                            tile_sum(T - 2, b, ONE_PLUS)
                        with dve.Else():
                            tile_sum(T - 2, b, MIXED)
                    elif not first:
                        tile_sum(T - 2, b, what)

                c = PLUS if what == ONE_PLUS else MINUS
                if what == MIXED:
                    dve.wait_ge(s_last, T * 4 + CREDIT["s_last"])
                    nc.vector.tensor_copy(psi_now[:, :, :], psi[:, :, :, bass.ds(T, 1)].rearrange("p c g o -> p c (g o)"))\
                      .then_inc(s_psi, 1)
                    dve.wait_ge(s_psi, T + 1)
                    for g in range(QUADS):
                        make_masks(T, g, what, PLUS)
                        if g:
                            turn(T, b, g - 1, what, PLUS)
                    sum_before()
                    turn(T, b, QUADS - 1, what, PLUS)
                else:
                    dve.sem_inc(s_psi, 1)
                    dve.sem_inc(s_first, QUADS)
                    dve.sem_inc(s_tfirst, QUADS)
                make_masks(T, 0, what, c)
                make_masks(T, 1, what, c)
                turn(T, b, 0, what, c)
                make_masks(T, 2, what, c)
                turn(T, b, 1, what, c)
                make_masks(T, 3, what, c)
                turn(T, b, 2, what, c)
                if what != MIXED:
                    sum_before()
                turn(T, b, 3, what, c)
                if not first:
                    numerator(T - 2, b)
                    result(T - 2, b, nth)

            def pair(G):
                for b in range(2):
                    by_kind(dve, G * 2 + b, lists, lambda what: tile(G * 2 + b, b, G, what))

            pair(0)
            pair(1)
            with dve.Fori(2, PAIRS) as G:
                pair(G)
            for b in range(2):
                S = TILES - 2 + b
                with dve.If(lists[1] < S + 1):
                    tile_sum(S, b, MIXED)
                with dve.Else():
                    tile_sum(S, b, ONE_PLUS)
                numerator(S, b)
                result(S, b, PAIRS)

        @block.tensor
        def _(pe):
            for name, semaphore in (("s_mlast", s_mlast), ("s_mfirst", s_mfirst), ("s_pick", s_pick)):
                pe.sem_inc(semaphore, CREDIT[name])
            pe.wait_ge(s_eye, 2)

            def turn_chunk(m, k):
                pe.wait_ge(s_norm, m + (k + 1))
                if not isinstance(m, int) or m + k >= RING:
                    pe.wait_ge(s_tc, m + (k + 1 - RING))
                for a in range(KK):
                    last = nc.tensor.transpose(bank[k % RING][:, a * P:(a + 1) * P], hn[:, k % RING, a * P:(a + 1) * P], ident)
                last.then_inc(s_tp, 1)

            def project(m, k):
                pe.wait_ge(s_tc, m + (k + 1))
                if not isinstance(m, int) or m + k >= RING:
                    pe.wait_ge(s_h, m + (k + 1 - RING))
                for a in range(KK):
                    last = nc.tensor.matmul(bank[RING + k % RING][:, 0:FE], hnT[:, k % RING, a, :], w1_sb[:, a, :],
                                            start=(a == 0), stop=(a == KK - 1))
                last.then_inc(s_hp, 1)

            turn_chunk(0, 0)
            pe.wait_ge(s_w, 1)
            for k in range(1, GX):
                turn_chunk(0, k)
                project(0, k - 1)
            with pe.Fori(1, GROUPS) as u:
                for k in range(GX):
                    turn_chunk(u * GX, k)
                    project(u * GX - GX, GX - 1) if k == 0 else project(u * GX, k - 1)
            project(CH - GX, GX - 1)
            pe.wait_ge(s_eye, 3 + 5 * QUADS + 3)
            pe.wait_ge(s_hs, CH)
            nc.tensor.matmul(bank[MEAN][:, 0:F], all_ones, hsum, start=True, stop=True).then_inc(s_mean, 1)
            pe.wait_ge(s_kind, 1)
            nc.tensor.matmul(bank[CUM][:, 0:3 * CH], lower, kind[:, :, :].rearrange("p k m -> p (k m)"), start=True, stop=True)
            nc.tensor.matmul(bank[CUM][:, 3 * CH:6 * CH], all_ones, kind[:, :, :].rearrange("p k m -> p (k m)"),
                             start=True, stop=True).then_inc(s_cum, 1)
            pe.wait_ge(s_spread, 1)
            for q in range(QN // 512):
                last = nc.tensor.matmul(bank[q][:, :], quad_ones,
                                        spread[:, 16 * q:16 * q + 16, :].rearrange("p m c -> p (m c)"), start=True, stop=True)
            last.then_inc(s_bc, 1)

            def take(o, j, start, stop):
                pe.wait_ge(s_onehot, j + 1)
                for k in range(HG):
                    last = nc.tensor.matmul(bank[ROWS][:, 0:2 * TILES], is_lo[:, o, k, :],
                                            picked[:, o, k, :, :].rearrange("p v t -> p (v t)"),
                                            start=start and k == 0, stop=stop and k == HG - 1)
                last.then_inc(s_pick, 1)

            for j in range(CH // HG):
                take(j % 2, j, j == 0, j == CH // HG - 1)
            for v, where in ((0, PICK_ROW), (1, PICK_PSI)):
                pe.wait_ge(s_slot, v + 1)
                for g in range(QUADS):
                    last = nc.tensor.matmul(bank[where][:, g * TILES:(g + 1) * TILES],
                                            pick[:, g, :, :].rearrange("p q r -> p (q r)"),
                                            row_s[:, 0, :] if v == 0 else row_psi[:, :], start=True, stop=True)
                last.then_inc(s_quads, 1)

            pe.wait_ge(s_lo, 2 * (CH // TB) + 1 + CREDIT["s_lo"])
            pe.wait_ge(s_gl, 1)
            pe.wait_ge(s_tau, 1)
            lists = list_ends(pe)

            def product(b, where, slot_, c, semaphore):
                for m in range(CH):
                    for a in range(2):
                        last = nc.tensor.matmul(acc[b][where][a][:, 0:FD], turned[:, slot_, m % PB, :, m // PB],
                                                tables[:, c, m, a, 0:FD], start=(m == 0), stop=(m == CH - 1))
                last.then_inc(semaphore, 1)

            def tile(T, b, what):
                pe.wait_ge(s_sum, T + (CREDIT["s_sum"] - 1))
                if what == MIXED:
                    wait_alone(pe, s_tfirst, T * 4 + 4)
                    product(b, 0, PLUS, PLUS, s_mfirst)
                    wait_alone(pe, s_tlast, T * 4 + (4 + CREDIT["s_tlast"]))
                    product(b, 1, MINUS, MINUS, s_mlast)
                else:
                    wait_alone(pe, s_tlast, T * 4 + (4 + CREDIT["s_tlast"]))
                    product(b, 0, b, PLUS if what == ONE_PLUS else MINUS, s_mlast)
                    pe.sem_inc(s_mfirst, 1)

            with pe.Fori(0, PAIRS) as G:
                for b in range(2):
                    by_kind(pe, G * 2 + b, lists, lambda what: tile(G * 2 + b, b, what))

def kernel(x, adj, L0_gnn_W1, L0_gnn_b1, L0_gnn_a1, L0_gnn_a2, L0_gnn_b2):
    import numpy as _np
    import concourse.bacc as _bacc
    from concourse import mybir as _mybir
    from concourse.bass_utils import run_bass_kernel_spmd as _run

    nc = _bacc.Bacc("TRN2", target_bir_lowering=False, num_devices=1, dynamic_dma_scratch_size=4096)
    given = {"x": x, "adj": adj, "w1": L0_gnn_W1, "b1": L0_gnn_b1, "a1": L0_gnn_a1, "a2": L0_gnn_a2, "b2": L0_gnn_b2}
    arrays, args = {}, []
    for name, value in given.items():
        a = _np.ascontiguousarray(value)
        if name == "b2":
            a = a.reshape(1)
        arrays[f"in_{name}"] = a
        args.append(nc.dram_tensor(f"in_{name}", a.shape, _mybir.dt.from_np(a.dtype), kind="ExternalInput").ap())
    out = nc.dram_tensor("out", given["x"].shape, F32, kind="ExternalOutput").ap()
    adjacency_attention(nc, *args, out)
    r = _run(nc, [arrays], core_ids=[0])
    return r.results[0]["out"]
```

```python
from contextlib import ExitStack

import concourse.bass as bass
from concourse import mybir

F32 = mybir.dt.float32
F16 = mybir.dt.float16
F8 = mybir.dt.float8e4
I32 = mybir.dt.int32
U32 = mybir.dt.uint32
ALU = mybir.AluOpType
ACT = mybir.ActivationFunctionType
AX_X = mybir.AxisListType.X
RMAX = bass.bass_isa.ReduceOp.max

P = 128
QUADS = 4
R = P // QUADS
ALPHA = 0.2
EPS = 1e-5
PLUS, MINUS = 0, 1
HIGH, LOW = 0, 1
LOW_SCALE = 4096.0
TABLE_SHIFT = 8.0 * 0.6931471805599453
ROUND = 12582912.0
MIXED, ONE_PLUS, ONE_MINUS = 0, 1, 2
MIXED_ODD = 3
ANY_MIXED = (MIXED, MIXED_ODD)
MARGIN = 2.0 ** -20
CREDIT = {"s_last": 4, "s_tlast": 4, "s_mlast": 2, "s_mfirst": 1, "s_sum": 2, "s_half": 1,
          "s_low": 2, "s_pick": 4}


def adjacency_attention(nc, x, adj, w1, b1, a1, a2, b2, out):
    N, F = x.shape
    QN = N // QUADS
    CH = QN // R
    FD = F + 1
    FE = F + 2
    KK = F // P
    PACK = 4
    PB = QN // (R * PACK)
    TILES = N // P
    PAIRS = TILES // 2
    GX = 8
    GROUPS = CH // GX
    RING = 4
    DEVIATION = 4
    TB = 4
    HG = 2 * TB
    STEPS = CH // TB
    SR = 4
    SORT = CH // HG

    x_rows = x.rearrange("(g n) f -> g n f", g=QUADS)
    adj_rows = adj.rearrange("n (q j) -> (n q) j", q=QUADS)

    ctx = ExitStack()
    with ctx:
        def sb(name, shape, dt):
            return ctx.enter_context(nc.sbuf_tensor(name, shape, dt))

        def sem(name):
            return ctx.enter_context(nc.semaphore(name))

        tables = sb("tables", [P, 2, CH, 2, FE], F16)
        h32 = tables[:, MINUS, :, :, :].rearrange("p m a f -> p m (a f)").bitcast(F32)
        early = tables[:, PLUS, :, :, :].rearrange("p m a f -> p (m a f)").bitcast(F32)
        xs = early[:, 0:2 * GX * F].rearrange("p (u k f) -> p u k f", u=2, k=GX)
        hn = early[:, 4096:4096 + RING * F].rearrange("p (k f) -> p k f", k=RING)
        hnT = early[:, 5120:5120 + RING * F].rearrange("p (k a i) -> p k a i", k=RING, a=KK)
        w1_sb = early[:, 6144:6144 + KK * FE].rearrange("p (a f) -> p a f", a=KK)
        a_bc = early[:, 6660:6660 + 2 * F].rearrange("p (a f) -> p a f", a=2)
        b_bc = early[:, 7172:7172 + FE]
        junk = early[:, 7430:7430 + F]

        adj_ring = sb("adj_ring", [P, QUADS, QN], I32)
        sorting = adj_ring[:, :, :].rearrange("p g j -> p (g j)").bitcast(F32)
        is_lo = sorting[:, 0:SR * HG * P].rearrange("p (s k i) -> p s k i", s=SR, k=HG)
        picked = sorting[:, 4096:4096 + 2 * SR * HG * TILES].rearrange("p (s k v t) -> p s k v t", s=SR, k=HG, v=2)

        tau = sb("tau", [P, QN], F32)
        work = sb("work", [P, 6 * 1024], F32)
        workb = work[:, :].bitcast(F8)
        masks = workb[:, 0:4 * QN].rearrange("p (g w e) -> p g w e", g=QUADS, e=PACK)
        turned = workb[:, 4 * QN:12 * QN].rearrange("p (s b i e) -> p s b i e", s=2, b=PB, e=PACK)
        is_hi = work[:, 0:SR * HG * TILES].rearrange("p (s k t) -> p s k t", s=SR, k=HG)
        spread = work[:, 2048:2048 + QN].rearrange("p (m c) -> p m c", c=R)
        ident = work[:, 4096:4096 + P]
        pick = work[:, 4224:4224 + QUADS * P].rearrange("p (g q r) -> p g q r", g=QUADS, q=QUADS)
        quad_ones = work[:, 4736:4736 + P]
        eye32 = work[:, 4864:4864 + R]
        all_ones = work[:, 4896:4896 + P]
        lower = work[:, 5024:5024 + P]
        count = work[:, 5152:5152 + P]
        row_no = work[:, 5280:5280 + CH]

        scaled = sb("scaled", [P, 2, TB, FD], F32)
        st = sb("st", [P, 2, CH], F32)
        late = sb("late", [P, 4 * FD + 6 * F], F32)
        parts = late[:, 0:4 * FD].rearrange("p (b c f) -> p b c f", b=2, c=2)
        xt = late[:, 4 * FD:4 * FD + 2 * F].rearrange("p (b f) -> p b f", b=2)
        ot = late[:, 4 * FD + 2 * F:4 * FD + 4 * F].rearrange("p (b f) -> p b f", b=2)
        ex = late[:, 4 * FD + 4 * F:4 * FD + 5 * F]
        pos = late[:, 4 * FD + 5 * F:4 * FD + 6 * F]
        taken = [0]

        def before(*dims):
            size = 1
            for d in dims:
                size *= d
            part = late[:, taken[0]:taken[0] + size]
            taken[0] += size
            axes = "abcd"[:len(dims)]
            if len(dims) == 1:
                return part
            return part.rearrange(f"p ({' '.join(axes)}) -> p {' '.join(axes)}", **dict(zip(axes[:-1], dims[:-1])))

        stats = before(2, GX, 6)
        mv = before(2, GX, 2)
        sd = before(2, GX)
        rstd = before(2, GX)
        shift = before(2, GX)
        hsum = before(F)
        grid = before(2, CH)
        grid2 = before(2, CH)
        kind = before(3, CH)
        total = before(3, CH)
        upto = before(3, CH)
        place = before(3, CH)
        zero = before(CH)
        step = before(2, CH)
        slot = before(4, CH)
        row_s = before(2, TILES)
        row_psi = before(TILES)
        tmp_t = before(TILES)
        hmean = sb("hmean", [P, F], F32)
        b2_bc = sb("b2_bc", [P, 1], F32)
        eps_col = sb("eps_col", [P, 1], F32)
        quad = sb("quad", [P, 1], F32)
        ends = sb("ends", [P, 2], F32)
        span = sb("span", [P, 2], F32)
        k0 = sb("k0", [P, 1], F32)
        k1 = sb("k1", [P, 1], F32)
        k2 = sb("k2", [P, 1], F32)
        ebias = sb("ebias", [P, 2], F32)
        full = sb("full", [P, 3], F32)
        full2 = sb("full2", [P, 3], F32)
        rest = sb("rest", [P, 3], F32)
        base = sb("base", [P, 1], F32)
        jump = sb("jump", [P, 3], F32)
        ends_i = sb("ends_i", [P, 3], I32)
        odd = sb("odd", [P, 3], F32)
        psi = sb("psi", [P, QUADS, TILES], F32)
        psi_now = sb("psi_now", [P, QUADS], F32)
        adj_idx = sb("adj_idx", [P, QUADS, TILES], U32)
        row_idx = sb("row_idx", [P, TILES], U32)
        adj_idx_now = sb("adj_idx_now", [P, 2, QUADS], U32)
        x_idx_now = sb("x_idx_now", [P, 2], U32)
        out_idx_now = sb("out_idx_now", [P, 2], U32)
        z = sb("z", [P, TILES], F32)
        gamma = sb("gamma", [P, TILES], F32)
        gamma_low = sb("gamma_low", [P, TILES], F32)
        fac = sb("fac", [P, 2, CH], F32)
        fac_low = sb("fac_low", [P, 2, CH], F32)
        flag = sb("flag", [P, 1], F32)
        den = sb("den", [P, 1], F32)
        rden = sb("rden", [P, 1], F32)

        acc = [[[ctx.enter_context(nc.psum_tensor(f"acc{b}{c}{a}", [P, 512], F32)) for a in range(2)]
                for c in range(2)] for b in range(2)]
        bank = [acc[b][c][a] for b in range(2) for c in range(2) for a in range(2)]
        ROWS, CUM, MEAN, PICK_ROW, PICK_PSI = 6, 7, 1, 4, 5
        SPREAD = (2, 3, 6, 7)

        s_const = sem("s_const")
        s_eye = sem("s_eye")
        s_x = [[sem(f"s_x{h}{k}") for k in range(GX)] for h in range(2)]
        s_norm = sem("s_norm")
        s_var = sem("s_var")
        s_sd = sem("s_sd")
        s_rs = sem("s_rs")
        s_tp = sem("s_tp")
        s_tc = sem("s_tc")
        s_hp = sem("s_hp")
        s_h = sem("s_h")
        s_w = sem("s_w")
        s_hs = sem("s_hs")
        s_mean = sem("s_mean")
        s_ends = sem("s_ends")
        s_span = sem("s_span")
        s_kind = sem("s_kind")
        s_cum = sem("s_cum")
        s_lists = sem("s_lists")
        s_spread = sem("s_spread")
        s_bc = sem("s_bc")
        s_tau = sem("s_tau")
        s_hot = sem("s_hot")
        s_picked = sem("s_picked")
        s_pick = sem("s_pick")
        s_slot = sem("s_slot")
        s_quads = sem("s_quads")
        s_idx = sem("s_idx")
        s_gam = sem("s_gam")
        s_gl = sem("s_gl")
        s_eb = sem("s_eb")
        s_exp = sem("s_exp")
        s_fac = sem("s_fac")
        s_sca = sem("s_sca")
        s_scp = sem("s_scp")
        s_hi = sem("s_hi")
        s_low = sem("s_low")
        s_adj = [sem(f"s_adj{g}") for g in range(QUADS)]
        s_first = sem("s_first")
        s_last = sem("s_last")
        s_psi = sem("s_psi")
        s_tfirst = sem("s_tfirst")
        s_tlast = sem("s_tlast")
        s_mfirst = sem("s_mfirst")
        s_mlast = sem("s_mlast")
        s_ic = sem("s_ic")
        s_xt = [sem(f"s_xt{b}") for b in range(2)]
        s_copy = sem("s_copy")
        s_mix = sem("s_mix")
        s_sum = sem("s_sum")
        s_tail = sem("s_tail")
        s_num = sem("s_num")
        s_elu = sem("s_elu")
        s_half = sem("s_half")
        s_ot = sem("s_ot")
        s_out = [sem(f"s_out{b}") for b in range(2)]
        s_passed = sem("s_passed")
        s_dve = sem("s_dve")

        def wait_alone(eng, semaphore, value):
            eng.wait_ge(semaphore, value)
            eng.sem_inc(s_passed, 1)

        def list_ends(eng):
            eng.wait_ge(s_lists, 1)
            return [eng.value_load(ends_i[0:1, k:k + 1], min_val=0, max_val=(TILES, TILES, 1)[k]) for k in range(3)]

        def by_kind(eng, T, lists, make, with_parity):
            with eng.If(T < lists[0]):
                make(ONE_PLUS)
            with eng.Else():
                with eng.If(T < lists[1]):
                    make(ONE_MINUS)
                with eng.Else():
                    if not with_parity:
                        make(MIXED)
                    else:
                        with eng.If(lists[2] < 1):
                            make(MIXED)
                        with eng.Else():
                            make(MIXED_ODD)

        def slot_of(b, what, c):
            if what in ANY_MIXED:
                return c if what == MIXED else 1 - c
            return b

        block = ctx.enter_context(nc.Block())

        @block.sync
        def _(sp):
            for k in range(GX):
                sp.dma_start(xs[:, 0, k, :], x_rows[:, k * R:(k + 1) * R, :]).then_inc(s_x[0][k], 16)
            sp.dma_start(w1_sb[:, :, 0:F], w1.rearrange("(a k) f -> k a f", a=KK)).then_inc(s_const, 16)
            sp.dma_start(a_bc[:, 0, :], a1.rearrange("(o f) -> o f", o=1).broadcast_to((P, F))).then_inc(s_const, 16)
            sp.dma_start(a_bc[:, 1, :], a2.rearrange("(o f) -> o f", o=1).broadcast_to((P, F))).then_inc(s_const, 16)
            sp.dma_start(b_bc[:, 0:F], b1.rearrange("(o f) -> o f", o=1).broadcast_to((P, F))).then_inc(s_const, 16)
            sp.dma_start(b2_bc[:, :], b2.rearrange("(o f) -> o f", o=1).broadcast_to((P, 1))).then_inc(s_const, 16)

            def load_group(u, half_, m0, after):
                for k in range(GX):
                    if after is not None:
                        sp.wait_ge(s_norm, after + k)
                    sp.dma_start(xs[:, half_, k, :], x_rows[:, bass.ds(m0 + k * R, R), :]).then_inc(s_x[half_][k], 16)

            load_group(1, 1, GX * R, None)
            with sp.Fori(1, GROUPS // 2) as v:
                for o in range(2):
                    load_group(None, o, v * (2 * GX * R) + o * GX * R, v * (2 * GX) + ((o - 2) * GX + 1))

        @block.gpsimd
        def _(pool):
            step = [0]

            def done(ins):
                step[0] += 1
                ins.then_inc(s_eye, 1)
                pool.wait_ge(s_eye, step[0])

            done(nc.gpsimd.memset(work[:, 4096:4896], 0.0))
            done(nc.gpsimd.affine_select(out=ident, in_=ident, compare_op=ALU.not_equal, fill=1.0, base=0,
                                         pattern=[[-1, P]], channel_multiplier=1))
            done(nc.gpsimd.memset(work[:, 4896:5152], 1.0))
            for g in range(QUADS):
                done(nc.gpsimd.affine_select(out=pick[:, g, :, :], in_=pick[:, g, :, :], compare_op=ALU.not_equal,
                                             fill=1.0, base=-R * g, pattern=[[0, QUADS], [-1, R]],
                                             channel_multiplier=1))
                done(nc.gpsimd.affine_select(out=eye32, in_=eye32, compare_op=ALU.not_equal, fill=1.0, base=-R * g,
                                             pattern=[[-1, R]], channel_multiplier=1))
                done(nc.gpsimd.memset(quad_ones[R * g:R * g + R, R * g:R * g + R], 1.0))
                done(nc.gpsimd.memset(quad[R * g:R * g + R, :], float(g)))
                done(nc.gpsimd.iota(row_no[R * g:R * g + R, :], pattern=[[R, CH]], base=QN * g, channel_multiplier=1,
                                    allow_small_or_imprecise_dtypes=True))
            done(nc.gpsimd.affine_select(out=lower, in_=lower, compare_op=ALU.is_gt, fill=0.0, base=0,
                                         pattern=[[1, P]], channel_multiplier=-1))
            done(nc.gpsimd.iota(count, pattern=[[1, P]], base=0, channel_multiplier=0,
                                allow_small_or_imprecise_dtypes=True))
            done(nc.gpsimd.memset(hsum, 0.0))
            pool.wait_ge(s_h, 1)
            nc.gpsimd.tensor_tensor(hsum, hsum, h32[:, 0, 0:F], ALU.add).then_inc(s_hs, 1)
            with pool.Fori(1, CH) as m:
                pool.wait_ge(s_h, m + 1)
                pool.wait_ge(s_hs, m)
                nc.gpsimd.tensor_tensor(hsum, hsum, h32[:, m, 0:F], ALU.add).then_inc(s_hs, 1)
            pool.wait_ge(s_ends, 1)
            nc.gpsimd.partition_all_reduce(span[:, :], ends[:, :], P, RMAX).then_inc(s_span, 1)

            def values(v, o):
                pool.wait_ge(s_hot, v * SR + (o + 1))
                m0 = v * (SR * HG) + o * HG
                for k, value in ((0, row_no[:, bass.ds(m0, HG)]), (1, st[:, 0, bass.ds(m0, HG)])):
                    last = nc.gpsimd.tensor_tensor(
                        picked[:, o, :, k, :], is_hi[:, o, :, :],
                        value.rearrange("p (k i) -> p k i", i=1).broadcast_to((P, HG, TILES)), ALU.mult)
                last.then_inc(s_picked, 1)

            def scale(v):
                m0 = v * HG + TB
                pool.wait_ge(s_low, v * 2 + CREDIT["s_low"])
                nc.gpsimd.tensor_tensor(
                    scaled[:, 1, :, 0:F], h32[:, bass.ds(m0, TB), 0:F],
                    fac_low[:, PLUS, bass.ds(m0, TB)].rearrange("p (k i) -> p k i", i=1).broadcast_to((P, TB, F)),
                    ALU.mult)
                nc.gpsimd.tensor_copy(scaled[:, 1, :, F], fac_low[:, PLUS, bass.ds(m0, TB)]).then_inc(s_scp, 1)

            pool.wait_ge(s_fac, 1)
            with pool.Fori(0, SORT // SR) as v:
                for o in range(0, SR, 2):
                    scale(v * (SR // 2) + o // 2)
                    values(v, o)
                    values(v, o + 1)
            scale(SORT // 2)

            pool.wait_ge(s_idx, 1)

            def set_out(T, b, x_too, out_too, G):
                if not isinstance(G, int) or G > 1:
                    wait_alone(pool, s_xt[b], G * 16 - 16)
                if not isinstance(G, int) or G + b > 2:
                    wait_alone(pool, s_out[1 - b], G * 16 + (b * 16 - 32))
                last = nc.gpsimd.tensor_copy(adj_idx_now[:, b, :], adj_idx[:, :, bass.ds(T, 1)].rearrange("p g o -> p (g o)"))
                last.then_inc(s_ic, 1)
                if x_too:
                    nc.gpsimd.tensor_copy(x_idx_now[:, b:b + 1], row_idx[:, bass.ds(T - 2, 1)]).then_inc(s_ic, 1)
                else:
                    pool.sem_inc(s_ic, 1)
                if out_too:
                    nc.gpsimd.tensor_copy(out_idx_now[:, 1 - b:2 - b], row_idx[:, bass.ds(T - 3, 1)]).then_inc(s_ic, 1)
                else:
                    pool.sem_inc(s_ic, 1)
                wait_alone(pool, s_ic, T * 3 + 3)

            def load_adj(T, b, slices=range(QUADS)):
                for g in slices:
                    wait_alone(pool, s_last, T * 4 + (g + 1))
                    nc.gpsimd.indirect_dma_start(adj_ring[:, g, :], None, adj_rows,
                                                 bass.IndirectOffsetOnAxis(ap=adj_idx_now[:, b, g:g + 1], axis=0))\
                      .then_inc(s_adj[g], 16)

            def load_x(b):
                nc.gpsimd.indirect_dma_start(xt[:, b, :], None, x,
                                             bass.IndirectOffsetOnAxis(ap=x_idx_now[:, b:b + 1], axis=0))\
                  .then_inc(s_xt[b], 16)

            def store(S, b):
                wait_alone(pool, s_ot, S + 1)
                nc.gpsimd.indirect_dma_start(out, bass.IndirectOffsetOnAxis(ap=out_idx_now[:, b:b + 1], axis=0),
                                             ot[:, b, :], None)\
                  .then_inc(s_out[b], 16)

            def pair(G, with_x, with_out):
                for b in range(2):
                    T = G * 2 + b
                    set_out(T, b, with_x, with_out[b], G)
                    load_adj(T, b)
                    if with_x:
                        load_x(b)
                    if with_out[b]:
                        store(T - 3, 1 - b)

            set_out(0, 0, False, False, 0)
            load_adj(0, 0, range(0, 2))
            scale(SORT // 2 + 1)
            load_adj(0, 0, range(2, QUADS))
            with pool.Fori(SORT // 2 + 2, STEPS // 2) as v:
                scale(v)
            set_out(1, 1, False, False, 0)
            load_adj(1, 1)
            pair(1, True, (False, True))
            pair(2, True, (True, True))
            with pool.Fori(3, PAIRS) as G:
                pair(G, True, (True, True))
            for b in range(2):
                pool.wait_ge(s_xt[b], (PAIRS - 1) * 16)
                pool.wait_ge(s_out[1 - b], (PAIRS - 2 + b) * 16)
                nc.gpsimd.tensor_copy(x_idx_now[:, b:b + 1], row_idx[:, TILES - 2 + b:TILES - 1 + b]).then_inc(s_ic, 1)
                nc.gpsimd.tensor_copy(out_idx_now[:, 1 - b:2 - b], row_idx[:, TILES - 3 + b:TILES - 2 + b]).then_inc(s_ic, 1)
                pool.wait_ge(s_ic, TILES * 3 + 2 * b + 2)
                load_x(b)
                store(TILES - 3 + b, 1 - b)
            pool.wait_ge(s_out[1], (PAIRS - 1) * 16)
            nc.gpsimd.tensor_copy(out_idx_now[:, 1:2], row_idx[:, TILES - 1:TILES]).then_inc(s_ic, 1)
            pool.wait_ge(s_ic, TILES * 3 + 5)
            store(TILES - 1, 1)
            for b in range(2):
                pool.wait_ge(s_out[b], PAIRS * 16)

        @block.scalar
        def _(act):
            act.wait_ge(s_dve, 1)
            nc.scalar.activation(flag[:, :], eps_col[:, :], ACT.Sqrt)

            def deviation(h):
                nc.scalar.activation(sd[:, h, :], mv[:, h, :, 1], ACT.Sqrt, bias=eps_col[:, :]).then_inc(s_sd, 1)

            def copy_turned(m, c):
                act.wait_ge(s_tp, m + (c + 1))
                if not isinstance(m, int) or m + c >= RING:
                    act.wait_ge(s_hp, m + (c + 1 - RING))
                nc.scalar.activation(hnT[:, c % RING, :, :], bank[c % RING][:, 0:F].rearrange("p (a i) -> p a i", a=KK),
                                     ACT.Copy).then_inc(s_tc, 1)

            def group(m, h, nth, use, final):
                act.wait_ge(s_rs, nth)
                for k in range(GX):
                    act.wait_ge(s_x[h][k], use * 16)
                    if not isinstance(m, int) or m + k >= RING:
                        act.wait_ge(s_tp, m + (k + 1 - RING))
                    nc.scalar.activation(hn[:, k % RING, :], xs[:, h, k, :], ACT.Relu, scale=rstd[:, h, k:k + 1],
                                         bias=shift[:, h, k:k + 1]).then_inc(s_norm, 1)
                    if k >= 1:
                        copy_turned(m, k - 1)
                    elif not isinstance(m, int) or m > 0:
                        copy_turned(m - GX, GX - 1)
                    if k == DEVIATION and not final:
                        act.wait_ge(s_var, nth + 1)
                        deviation(1 - h)
                if final:
                    copy_turned(m, GX - 1)

            act.wait_ge(s_var, 1)
            deviation(0)
            group(0, 0, 1, 1, False)
            group(GX, 1, 2, 1, False)
            with act.Fori(1, GROUPS // 2 - 1) as v:
                for o in range(2):
                    group(v * (2 * GX) + o * GX, o, v * 2 + (o + 1), v + 1, False)
            group(CH - 2 * GX, 0, GROUPS - 1, GROUPS // 2, False)
            group(CH - GX, 1, GROUPS, GROUPS // 2, True)

            nc.scalar.activation(den[:, :], eps_col[:, :], ACT.Exp)
            act.wait_ge(s_eb, 1)
            nc.scalar.activation(fac[:, PLUS, :], st[:, 1, :], ACT.Exp, bias=ebias[:, 0:1])
            nc.scalar.activation(fac[:, MINUS, :], st[:, 1, :], ACT.Exp, bias=ebias[:, 1:2], scale=ALPHA).then_inc(s_exp, 1)

            def scale(c, j, m0, o, nth):
                act.wait_ge(s_low, j + (CREDIT["s_low"] - 1))
                for k in range(TB):
                    nc.scalar.activation(scaled[:, o, k, 0:F], h32[:, m0 + k, 0:F], ACT.Copy,
                                         scale=fac_low[:, c, bass.ds(m0 + k, 1)])
                nc.scalar.activation(scaled[:, o, :, F], fac_low[:, c, bass.ds(m0, TB)], ACT.Copy).then_inc(s_sca, 1)
                act.wait_ge(s_sca, nth)

            def high(c, m0, o):
                nc.scalar.activation(tables[:, c, bass.ds(m0, TB), HIGH, 0:FD], scaled[:, o, :, :],
                                     ACT.Copy, scale=1.0 / LOW_SCALE).then_inc(s_hi, 1)

            def y_step(v, o):
                scale(MINUS, v * 2 + (STEPS + o), v * HG + o * TB, o, v * 2 + (STEPS // 2 + o + 1))
                high(MINUS, v * HG + o * TB, o)

            act.wait_ge(s_fac, 1)

            def x_steps(v):
                scale(PLUS, v * 2, v * HG, 0, v + 1)
                high(PLUS, v * HG, 0)
                act.wait_ge(s_scp, v + 1)
                high(PLUS, v * HG + TB, 1)

            with act.Fori(0, SORT // 2 + 2) as v:
                x_steps(v)
            act.wait_ge(s_slot, 2)
            nc.scalar.activation(gamma[:, :], z[:, :], ACT.Exp, scale=-(1.0 - ALPHA)).then_inc(s_gam, 1)
            with act.Fori(SORT // 2 + 2, STEPS // 2) as v:
                x_steps(v)
            act.wait_ge(s_bc, 1)
            for q in range(QN // 512):
                last = nc.scalar.activation(tau[:, 512 * q:512 * q + 512], bank[SPREAD[q]][:, :], ACT.Copy)
            last.then_inc(s_tau, 1)

            lists = list_ends(act)
            act.wait_ge(s_gam, 1)

            def tile(T, b, what):
                act.wait_ge(s_mlast, T + (1 + CREDIT["s_mlast"]))
                act.wait_ge(s_sum, T + (CREDIT["s_sum"] - 1))
                first = nc.scalar.activation(parts[:, b, 0, :], acc[b][0][HIGH][:, 0:FD], ACT.Copy)
                if what in ANY_MIXED:
                    nc.scalar.activation(parts[:, b, 1, :], acc[b][1][HIGH][:, 0:FD], ACT.Copy,
                                         scale=gamma[:, bass.ds(T, 1)]).then_inc(s_copy, 1)
                else:
                    first.then_inc(s_copy, 1)
                act.wait_ge(s_num, T + 1)
                act.wait_ge(s_half, T + CREDIT["s_half"])
                nc.scalar.activation(ex, parts[:, b, 0, 0:F], ACT.Exp, scale=rden[:, :])
                nc.scalar.activation(pos, parts[:, b, 0, 0:F], ACT.Relu, scale=rden[:, :]).then_inc(s_elu, 1)

            def pair(G):
                for b in range(2):
                    by_kind(act, G * 2 + b, lists, lambda what: tile(G * 2 + b, b, what), False)

            with act.If(lists[0] < STEPS):
                with act.Fori(0, STEPS // 2) as v:
                    for o in range(2):
                        y_step(v, o)
                with act.Fori(0, STEPS // 2) as G:
                    pair(G)
            with act.Else():
                with act.Fori(0, STEPS // 2) as G:
                    for o in range(2):
                        y_step(G, o)
                    for b in range(2):
                        tile(G * 2 + b, b, ONE_PLUS)
            with act.Fori(STEPS // 2, PAIRS) as G:
                pair(G)

        @block.vector
        def _(dve):
            chain = [0]

            def put(ins):
                chain[0] += 1
                ins.then_inc(s_dve, 1)

            def link(ins):
                chain[0] += 1
                ins.then_inc(s_dve, 1)
                dve.wait_ge(s_dve, chain[0])

            for name, semaphore in (("s_last", s_last), ("s_tlast", s_tlast), ("s_sum", s_sum),
                                    ("s_half", s_half), ("s_low", s_low)):
                dve.sem_inc(semaphore, CREDIT[name])
            link(nc.vector.memset(eps_col[:, :], EPS))
            link(nc.vector.memset(zero[:, :], 0.0))

            def statistics(h, use, n0):
                for k in range(GX):
                    dve.wait_ge(s_x[h][k], use * 16)
                    nc.vector.bn_stats(stats[:, h, k, :], xs[:, h, k, :]).then_inc(s_dve, 1)
                wait_alone(dve, s_dve, n0 + GX)
                for k in range(GX):
                    last = nc.vector.bn_aggr(mv[:, h, k, :], stats[:, h, k, :])
                    last.then_inc(s_var if k == GX - 1 else s_dve, 1)

            def scale_and_shift(h, nth, n0):
                dve.wait_ge(s_sd, nth)
                nc.vector.reciprocal(rstd[:, h, :], sd[:, h, :]).then_inc(s_dve, 1)
                dve.wait_ge(s_dve, n0 + 2 * GX)
                nc.vector.scalar_tensor_tensor(out=shift[:, h, :], in0=mv[:, h, :, 0], scalar=-1.0, in1=rstd[:, h, :],
                                               op0=ALU.mult, op1=ALU.mult).then_inc(s_rs, 1)

            def store_h(m, k):
                dve.wait_ge(s_hp, m + (k + 1))
                nc.vector.tensor_tensor(h32[:, m + k, 0:FE], bank[RING + k % RING][:, 0:FE], b_bc, ALU.add).then_inc(s_h, 1)

            def group(m, h, nth, use, n0, final):
                if not final:
                    statistics(1 - h, use + h, n0 + 2 * GX)
                for k in range(DEVIATION + 1):
                    store_h(m, k)
                if not final:
                    scale_and_shift(1 - h, nth + 1, n0 + 2 * GX)
                for k in range(DEVIATION + 1, GX):
                    store_h(m, k)

            C0 = chain[0]
            statistics(0, 1, C0)
            scale_and_shift(0, 1, C0)
            chain[0] += 2 * GX
            dve.wait_ge(s_const, 80)
            for c in range(2):
                for a in range(KK):
                    link(nc.vector.scalar_tensor_tensor(out=junk, in0=w1_sb[:, a, 0:F], scalar=1.0, in1=a_bc[:, c, :],
                                                        op0=ALU.mult, op1=ALU.mult,
                                                        accum_out=w1_sb[:, a, F + c:F + c + 1]))
                link(nc.vector.scalar_tensor_tensor(out=junk, in0=b_bc[:, 0:F], scalar=1.0, in1=a_bc[:, c, :],
                                                    op0=ALU.mult, op1=ALU.mult, accum_out=b_bc[:, F + c:F + c + 1]))
            nc.vector.tensor_tensor(b_bc[:, F:F + 1], b_bc[:, F:F + 1], b2_bc[:, :], ALU.add).then_inc(s_w, 1)
            dve.wait_ge(s_w, 1)
            D0 = chain[0] - 2 * GX
            group(0, 0, 1, 1, D0, False)
            group(GX, 1, 2, 1, D0 + 2 * GX, False)
            with dve.Fori(1, GROUPS // 2 - 1) as v:
                for o in range(2):
                    group(v * (2 * GX) + o * GX, o, v * 2 + (o + 1), v + 1, v * (4 * GX) + (D0 + o * 2 * GX), False)
            group(CH - 2 * GX, 0, GROUPS - 1, GROUPS // 2, D0 + 2 * GX * (GROUPS - 2), False)
            group(CH - GX, 1, GROUPS, GROUPS // 2, None, True)
            chain[0] = D0 + 2 * GX * GROUPS

            dve.wait_ge(s_h, CH)
            link(nc.vector.tensor_copy(st[:, :, :], h32[:, :, F:FE].rearrange("p m c -> p c m")))
            put(nc.vector.tensor_reduce(ends[:, 0:1], st[:, 1, :], AX_X, ALU.max))
            link(nc.vector.tensor_reduce(ends[:, 1:2], st[:, 1, :], AX_X, ALU.min))
            nc.vector.tensor_scalar(ends[:, 1:2], ends[:, 1:2], -1.0, None, ALU.mult).then_inc(s_ends, 1)
            dve.wait_ge(s_span, 1)
            put(nc.vector.tensor_scalar(ebias[:, 0:1], span[:, 0:1], -1.0, TABLE_SHIFT, ALU.mult, ALU.add))
            nc.vector.tensor_scalar(ebias[:, 1:2], span[:, 0:1], -ALPHA, TABLE_SHIFT, ALU.mult, ALU.add).then_inc(s_eb, 1)
            link(nc.vector.tensor_tensor(k0[:, :], span[:, 0:1], span[:, 1:2], ALU.add))
            link(nc.vector.tensor_scalar(k1[:, :], k0[:, :], 2.0, 1e-30, ALU.mult, ALU.max))
            link(nc.vector.reciprocal(k2[:, :], k1[:, :]))

            def threshold(dst, src, tmp):
                link(nc.vector.tensor_scalar(dst, src, span[:, 0:1], k2[:, :], ALU.add, ALU.mult))
                link(nc.vector.tensor_scalar(tmp, dst, -0.125, 0.625, ALU.max, ALU.min))
                link(nc.vector.tensor_scalar(dst, tmp, 1.25, -1.0, ALU.add, ALU.add))

            threshold(grid[:, 0, :], st[:, 0, :], grid2[:, 0, :])
            put(nc.vector.tensor_scalar(kind[:, ONE_PLUS, :], grid[:, 0, :], 0.75 + MARGIN, None, ALU.is_gt))
            link(nc.vector.tensor_scalar(kind[:, ONE_MINUS, :], grid[:, 0, :], 0.25 - MARGIN, None, ALU.is_lt))
            link(nc.vector.tensor_tensor(grid2[:, 0, :], kind[:, ONE_PLUS, :], kind[:, ONE_MINUS, :], ALU.add))
            nc.vector.tensor_scalar(kind[:, MIXED, :], grid2[:, 0, :], -1.0, 1.0, ALU.mult, ALU.add).then_inc(s_kind, 1)
            dve.wait_ge(s_exp, 1)
            nc.vector.tensor_scalar(fac_low[:, :, :], fac[:, :, :], LOW_SCALE, None, ALU.mult).then_inc(s_fac, 1)
            dve.wait_ge(s_cum, 1)
            link(nc.vector.tensor_copy(total[:, :, :], bank[CUM][:, 3 * CH:6 * CH].rearrange("p (k m) -> p k m", k=3)))
            for k in range(3):
                scan = nc.vector.tensor_tensor_scan(upto[:, k, :], total[:, k, :], zero[:, :], 0.0, ALU.add, ALU.add)
                link(scan) if k == 2 else put(scan)
            link(nc.vector.tensor_scalar(full2[:, :], upto[:, :, CH - 1], 1.0 / P, -0.498, ALU.mult, ALU.add))
            link(nc.vector.tensor_scalar(full2[:, :], full2[:, :], ROUND, -ROUND, ALU.add, ALU.add))
            put(nc.vector.tensor_copy(ends_i[:, 0:1], full2[:, ONE_PLUS:ONE_PLUS + 1]))
            nc.vector.tensor_tensor(ends_i[:, 1:2], full2[:, ONE_PLUS:ONE_PLUS + 1], full2[:, ONE_MINUS:ONE_MINUS + 1],
                                    ALU.add).then_inc(s_dve, 1)
            chain[0] += 1
            link(nc.vector.tensor_scalar(full[:, :], full2[:, :], float(P), None, ALU.mult))
            put(nc.vector.tensor_tensor(rest[:, :], upto[:, :, CH - 1], full[:, :], ALU.subtract))
            put(nc.vector.tensor_tensor(base[:, :], full[:, ONE_PLUS:ONE_PLUS + 1],
                                         full[:, ONE_MINUS:ONE_MINUS + 1], ALU.add))
            link(nc.vector.tensor_tensor(place[:, :, :], upto[:, :, :], total[:, :, :], ALU.subtract))
            put(nc.vector.tensor_tensor(jump[:, ONE_PLUS:ONE_PLUS + 1], full[:, ONE_MINUS:ONE_MINUS + 1],
                                         upto[:, MIXED, CH - 1:CH], ALU.add))
            link(nc.vector.tensor_tensor(jump[:, ONE_MINUS:ONE_MINUS + 1], rest[:, ONE_PLUS:ONE_PLUS + 1],
                                         upto[:, MIXED, CH - 1:CH], ALU.add))
            link(nc.vector.tensor_tensor(upto[:, :, :], place[:, :, :],
                                         bank[CUM][:, 0:3 * CH].rearrange("p (k m) -> p k m", k=3), ALU.add))
            for k in (ONE_PLUS, ONE_MINUS):
                put(nc.vector.tensor_scalar(step[:, k - 1, :], upto[:, k, :], full[:, k:k + 1], jump[:, k:k + 1],
                                            ALU.is_ge, ALU.mult))
            link(nc.vector.tensor_scalar(place[:, MIXED, :], upto[:, MIXED, :], base[:, :], None, ALU.add))
            put(nc.vector.tensor_tensor(place[:, ONE_PLUS, :], upto[:, ONE_PLUS, :], step[:, 0, :], ALU.add))
            link(nc.vector.scalar_tensor_tensor(out=place[:, ONE_MINUS, :], in0=upto[:, ONE_MINUS, :],
                                                scalar=full[:, ONE_PLUS:ONE_PLUS + 1], in1=step[:, 1, :],
                                                op0=ALU.add, op1=ALU.add))
            link(nc.vector.tensor_tensor(upto[:, :, :], place[:, :, :], kind[:, :, :], ALU.mult))
            link(nc.vector.tensor_tensor(slot[:, 0, :], upto[:, 0, :], upto[:, 1, :], ALU.add))
            link(nc.vector.tensor_tensor(slot[:, 1, :], slot[:, 0, :], upto[:, 2, :], ALU.add))
            link(nc.vector.tensor_scalar(slot[:, 0, :], slot[:, 1, :], 1.0 / P, -0.498, ALU.mult, ALU.add))
            link(nc.vector.tensor_scalar(slot[:, 2, :], slot[:, 0, :], ROUND, -ROUND, ALU.add, ALU.add))
            link(nc.vector.scalar_tensor_tensor(out=slot[:, 3, :], in0=slot[:, 2, :], scalar=-float(P), in1=slot[:, 1, :],
                                                op0=ALU.mult, op1=ALU.add))


            def rows_to_slots(v, o, j):
                m0 = v * (SR * HG) + o * HG
                wait_alone(dve, s_pick, j + (CREDIT["s_pick"] - (SR - 1)))
                nc.vector.tensor_tensor(
                    is_lo[:, o, :, :], slot[:, 3, bass.ds(m0, HG)].rearrange("p (k i) -> p k i", i=1).broadcast_to((P, HG, P)),
                    count.rearrange("p (k i) -> p k i", k=1).broadcast_to((P, HG, P)), ALU.is_equal)
                nc.vector.tensor_tensor(
                    is_hi[:, o, :, :], slot[:, 2, bass.ds(m0, HG)].rearrange("p (k i) -> p k i", i=1).broadcast_to((P, HG, TILES)),
                    count[:, 0:TILES].rearrange("p (k i) -> p k i", k=1).broadcast_to((P, HG, TILES)), ALU.is_equal)\
                  .then_inc(s_hot, 1)

            def table_low(c, v, o, j):
                m0 = v * HG + o * TB
                dve.wait_ge(s_hi, j + 1)
                nc.vector.scalar_tensor_tensor(out=tables[:, c, bass.ds(m0, TB), LOW, 0:FD],
                                               in0=tables[:, c, bass.ds(m0, TB), HIGH, 0:FD], scalar=-LOW_SCALE,
                                               in1=scaled[:, o, :, :], op0=ALU.mult, op1=ALU.add).then_inc(s_low, 1)

            with dve.Fori(0, SORT // SR) as v:
                for o in range(SR):
                    rows_to_slots(v, o, v * SR + o)
                    table_low(PLUS, v * (SR // 2) + o // 2, o % 2, v * SR + o)

            link(nc.vector.tensor_scalar(grid2[:, 1, :], st[:, 1, :], -1.0, None, ALU.mult))
            threshold(grid[:, 1, :], grid2[:, 1, :], grid2[:, 0, :])
            link(nc.vector.tensor_tensor(odd[:, 0:1], full2[:, ONE_PLUS:ONE_PLUS + 1], full2[:, ONE_MINUS:ONE_MINUS + 1],
                                         ALU.add))
            link(nc.vector.tensor_scalar(odd[:, 1:2], odd[:, 0:1], 0.5, -0.25, ALU.mult, ALU.add))
            link(nc.vector.tensor_scalar(odd[:, 2:3], odd[:, 1:2], ROUND, -ROUND, ALU.add, ALU.add))
            nc.vector.scalar_tensor_tensor(out=ends_i[:, 2:3], in0=odd[:, 2:3], scalar=-2.0, in1=odd[:, 0:1],
                                           op0=ALU.mult, op1=ALU.add).then_inc(s_lists, 1)
            dve.wait_ge(s_mean, 1)
            link(nc.vector.tensor_scalar(hmean[:, :], bank[MEAN][:, 0:F], 1.0 / N, None, ALU.mult))
            lists = list_ends(dve)

            dve.wait_ge(s_pick, CH // HG + CREDIT["s_pick"])
            nc.vector.tensor_copy(row_s[:, :, :], bank[ROWS][:, 0:2 * TILES].rearrange("p (v t) -> p v t", v=2))\
              .then_inc(s_slot, 1)
            dve.wait_ge(s_slot, 1)
            nc.vector.tensor_copy(row_idx[:, :], row_s[:, 0, :])
            nc.vector.tensor_tensor(spread[:, :, :], grid[:, 1, :].rearrange("p (m o) -> p m o", o=1).broadcast_to((P, CH, R)),
                                    eye32.rearrange("p (o c) -> p o c", o=1).broadcast_to((P, CH, R)), ALU.mult)\
              .then_inc(s_spread, 1)
            dve.wait_ge(s_quads, 1)
            nc.vector.tensor_scalar(adj_idx[:, :, :], bank[PICK_ROW][:, 0:QUADS * TILES].rearrange("p (g t) -> p g t", g=QUADS),
                                    float(QUADS), quad[:, :], ALU.mult, ALU.add).then_inc(s_idx, 1)
            for o in range(2):
                table_low(PLUS, SORT // 2, o, SORT + o)
            threshold(row_psi[:, :], row_s[:, 1, :], tmp_t[:, :])
            nc.vector.tensor_scalar(z[:, :], row_s[:, 1, :], span[:, 0:1], 0.0, ALU.add, ALU.max).then_inc(s_slot, 1)
            dve.wait_ge(s_quads, 2)
            psi_q = bank[PICK_PSI][:, 0:QUADS * TILES].rearrange("p (g t) -> p g t", g=QUADS)
            nc.vector.tensor_scalar(psi[:, :, :], psi_q, 1.0, None, ALU.mult).then_inc(s_psi, 1)
            for o in range(2):
                table_low(PLUS, SORT // 2 + 1, o, SORT + 2 + o)

            def gammas():
                dve.wait_ge(s_gam, 1)
                nc.vector.tensor_scalar(gamma_low[:, :], gamma[:, :], 1.0 / LOW_SCALE, None, ALU.mult).then_inc(s_gl, 1)

            def make_masks(T, g, what, c):
                dst = masks[:, g, :, :].rearrange("p w e -> p e w")
                src = adj_ring[:, g, :].rearrange("p (e w) -> p e w", e=PACK)
                if c == PLUS or what not in ANY_MIXED:
                    wait_alone(dve, s_adj[g], T * 16 + 16)
                    wait_alone(dve, s_tlast, T * 4 + (g + 1))
                else:
                    wait_alone(dve, s_tfirst, T * 4 + (g + 1))
                if what in ANY_MIXED:
                    if c == PLUS:
                        nc.vector.scalar_tensor_tensor(out=dst, in0=src, scalar=psi_now[:, g:g + 1],
                                                       in1=tau[:, :].rearrange("p (e w) -> p e w", e=PACK), op0=ALU.min,
                                                       op1=ALU.is_gt, saturate=False).then_inc(s_first, 1)
                    else:
                        nc.vector.scalar_tensor_tensor(out=dst, in0=src, scalar=0.0, in1=dst, op0=ALU.is_gt,
                                                       op1=ALU.subtract, saturate=False).then_inc(s_last, 1)
                else:
                    nc.vector.tensor_scalar(dst, src, 0, None, ALU.is_gt, saturate=False).then_inc(s_last, 1)

            def turn(T, b, g, what, c):
                early_class = what in ANY_MIXED and c == PLUS
                if g == 0:
                    if early_class:
                        with dve.If(lists[1] < T):
                            wait_alone(dve, s_mfirst, T + CREDIT["s_mfirst"])
                        with dve.Else():
                            wait_alone(dve, s_mlast, T + (CREDIT["s_mlast"] - 1))
                    elif what in ANY_MIXED:
                        dve.wait_ge(s_mlast, T + CREDIT["s_mlast"])
                    else:
                        dve.wait_ge(s_mlast, T + (CREDIT["s_mlast"] - 1))
                if early_class:
                    dve.wait_ge(s_first, T * 4 + (g + 1))
                else:
                    dve.wait_ge(s_last, T * 4 + (g + 1 + CREDIT["s_last"]))
                where = slot_of(b, what, c)
                nc.vector.transpose(
                    turned[:, where, :, R * g:R * g + R, :].rearrange("p b r e -> p b (r e)").bitcast(U32),
                    masks[:, g, :, :].rearrange("p (b c) e -> p b (c e)", b=PB).bitcast(U32))\
                  .then_inc(s_tfirst if early_class else s_tlast, 1)

            def tile_sum(S, b, what):
                dve.wait_ge(s_copy, S + 1)
                if what in ANY_MIXED:
                    nc.vector.scalar_tensor_tensor(out=parts[:, b, 0, :], in0=acc[b][0][LOW][:, 0:FD], scalar=1.0 / LOW_SCALE,
                                                   in1=parts[:, b, 0, :], op0=ALU.mult, op1=ALU.add).then_inc(s_mix, 1)
                    nc.vector.scalar_tensor_tensor(out=parts[:, b, 1, :], in0=acc[b][1][LOW][:, 0:FD],
                                                   scalar=gamma_low[:, bass.ds(S, 1)], in1=parts[:, b, 1, :],
                                                   op0=ALU.mult, op1=ALU.add).then_inc(s_mix, 1)
                    dve.wait_ge(s_mix, S * 2 + 2)
                    nc.vector.tensor_tensor(parts[:, b, 0, :], parts[:, b, 0, :], parts[:, b, 1, :], ALU.add).then_inc(s_sum, 1)
                else:
                    dve.sem_inc(s_mix, 2)
                    nc.vector.scalar_tensor_tensor(out=parts[:, b, 0, :], in0=acc[b][0][LOW][:, 0:FD], scalar=1.0 / LOW_SCALE,
                                                   in1=parts[:, b, 0, :], op0=ALU.mult, op1=ALU.add).then_inc(s_sum, 1)

            def numerator(S, b):
                dve.wait_ge(s_sum, S + (1 + CREDIT["s_sum"]))
                nc.vector.tensor_scalar(flag[:, :], parts[:, b, 0, F:FD], 0.0, None, ALU.is_equal).then_inc(s_tail, 1)
                dve.wait_ge(s_tail, S * 3 + 1)
                nc.vector.tensor_tensor(den[:, :], parts[:, b, 0, F:FD], flag[:, :], ALU.add).then_inc(s_tail, 1)
                dve.wait_ge(s_tail, S * 3 + 2)
                nc.vector.reciprocal(rden[:, :], den[:, :]).then_inc(s_tail, 1)
                nc.vector.scalar_tensor_tensor(out=parts[:, b, 0, 0:F], in0=hmean[:, :], scalar=flag[:, :],
                                               in1=parts[:, b, 0, 0:F], op0=ALU.mult, op1=ALU.add).then_inc(s_num, 1)

            def result(S, b, nth):
                dve.wait_ge(s_elu, S + 1)
                if not isinstance(nth, int) or nth > 1:
                    dve.wait_ge(s_out[b], nth * 16 - 16)
                nc.vector.scalar_tensor_tensor(out=ot[:, b, :], in0=ex, scalar=1.0, in1=pos,
                                               op0=ALU.min, op1=ALU.add).then_inc(s_half, 1)
                dve.wait_ge(s_half, S + (1 + CREDIT["s_half"]))
                dve.wait_ge(s_xt[b], nth * 16)
                nc.vector.scalar_tensor_tensor(out=ot[:, b, :], in0=ot[:, b, :], scalar=-1.0, in1=xt[:, b, :],
                                               op0=ALU.add, op1=ALU.add).then_inc(s_ot, 1)

            def tile(T, b, nth, what):
                first = isinstance(nth, int) and nth == 0

                def sum_before():
                    if not first and what in ANY_MIXED:
                        with dve.If(T < lists[1] + 2):
                            tile_sum(T - 2, b, ONE_PLUS)
                        with dve.Else():
                            tile_sum(T - 2, b, MIXED)
                    elif not first:
                        tile_sum(T - 2, b, what)

                c = PLUS if what == ONE_PLUS else MINUS
                if what in ANY_MIXED:
                    dve.wait_ge(s_last, T * 4 + CREDIT["s_last"])
                    dve.wait_ge(s_psi, T + 1)
                    nc.vector.tensor_copy(psi_now[:, :], psi[:, :, bass.ds(T, 1)].rearrange("p g o -> p (g o)"))\
                      .then_inc(s_psi, 1)
                    dve.wait_ge(s_psi, T + 2)
                    for g in range(QUADS):
                        make_masks(T, g, what, PLUS)
                        if g:
                            turn(T, b, g - 1, what, PLUS)
                    sum_before()
                    turn(T, b, QUADS - 1, what, PLUS)
                else:
                    dve.sem_inc(s_psi, 1)
                    dve.sem_inc(s_first, QUADS)
                    dve.sem_inc(s_tfirst, QUADS)
                make_masks(T, 0, what, c)
                make_masks(T, 1, what, c)
                turn(T, b, 0, what, c)
                make_masks(T, 2, what, c)
                turn(T, b, 1, what, c)
                make_masks(T, 3, what, c)
                turn(T, b, 2, what, c)
                if what not in ANY_MIXED:
                    sum_before()
                turn(T, b, 3, what, c)
                if not first:
                    numerator(T - 2, b)
                    result(T - 2, b, nth)

            def pair(G):
                for b in range(2):
                    by_kind(dve, G * 2 + b, lists, lambda what: tile(G * 2 + b, b, G, what), True)

            with dve.If(lists[0] < STEPS):
                with dve.Fori(SORT // 2 + 2, STEPS // 2) as v:
                    for o in range(2):
                        table_low(PLUS, v, o, v * 2 + o)
                gammas()
                dve.wait_ge(s_bc, 1)
                dve.wait_ge(s_gl, 1)
                dve.wait_ge(s_tau, 1)
                with dve.Fori(0, STEPS // 2) as v:
                    for o in range(2):
                        table_low(MINUS, v, o, v * 2 + (STEPS + o))
                pair(0)
                pair(1)
                with dve.Fori(2, STEPS // 2) as G:
                    pair(G)
            with dve.Else():
                dve.sem_inc(s_psi, 1)
                dve.sem_inc(s_first, QUADS)
                dve.sem_inc(s_tfirst, QUADS)
                for g in range(QUADS):
                    v = SORT // 2 + g
                    if g >= 2:
                        table_low(PLUS, v, 0, 2 * v)
                        table_low(PLUS, v, 1, 2 * v + 1)
                    make_masks(0, g, ONE_PLUS, PLUS)
                    if g == 1:
                        dve.wait_ge(s_bc, 1)
                    if g == 2:
                        gammas()
                    if g >= 1:
                        turn(0, 0, g - 1, ONE_PLUS, PLUS)
                turn(0, 0, QUADS - 1, ONE_PLUS, PLUS)
                dve.wait_ge(s_gl, 1)
                dve.wait_ge(s_tau, 1)
                tile(1, 1, 0, ONE_PLUS)

                def pair_and_y(G):
                    for b in range(2):
                        tile(G * 2 + b, b, G, ONE_PLUS)
                        table_low(MINUS, G - 1, b, G * 2 + (STEPS - 2 + b))

                pair_and_y(1)
                with dve.Fori(2, STEPS // 2) as G:
                    pair_and_y(G)
                for b in range(2):
                    table_low(MINUS, STEPS // 2 - 1, b, 2 * STEPS - 2 + b)
            with dve.Fori(STEPS // 2, PAIRS) as G:
                pair(G)
            for b in range(2):
                S = TILES - 2 + b
                with dve.If(lists[1] < S + 1):
                    tile_sum(S, b, MIXED)
                with dve.Else():
                    tile_sum(S, b, ONE_PLUS)
                numerator(S, b)
                result(S, b, PAIRS)

        @block.tensor
        def _(pe):
            for name, semaphore in (("s_mlast", s_mlast), ("s_mfirst", s_mfirst), ("s_pick", s_pick)):
                pe.sem_inc(semaphore, CREDIT[name])
            pe.wait_ge(s_eye, 2)

            def turn_chunk(m, k):
                pe.wait_ge(s_norm, m + (k + 1))
                if not isinstance(m, int) or m + k >= RING:
                    pe.wait_ge(s_tc, m + (k + 1 - RING))
                for a in range(KK):
                    last = nc.tensor.transpose(bank[k % RING][:, a * P:(a + 1) * P], hn[:, k % RING, a * P:(a + 1) * P], ident)
                last.then_inc(s_tp, 1)

            def project(m, k):
                pe.wait_ge(s_tc, m + (k + 1))
                if not isinstance(m, int) or m + k >= RING:
                    pe.wait_ge(s_h, m + (k + 1 - RING))
                for a in range(KK):
                    last = nc.tensor.matmul(bank[RING + k % RING][:, 0:FE], hnT[:, k % RING, a, :], w1_sb[:, a, :],
                                            start=(a == 0), stop=(a == KK - 1))
                last.then_inc(s_hp, 1)

            turn_chunk(0, 0)
            pe.wait_ge(s_w, 1)
            for k in range(1, GX):
                turn_chunk(0, k)
                project(0, k - 1)
            with pe.Fori(1, GROUPS) as u:
                for k in range(GX):
                    turn_chunk(u * GX, k)
                    project(u * GX - GX, GX - 1) if k == 0 else project(u * GX, k - 1)
            project(CH - GX, GX - 1)
            pe.wait_ge(s_eye, 3 + 5 * QUADS + 3)
            pe.wait_ge(s_hs, CH)
            nc.tensor.matmul(bank[MEAN][:, 0:F], all_ones, hsum, start=True, stop=True).then_inc(s_mean, 1)
            pe.wait_ge(s_kind, 1)
            nc.tensor.matmul(bank[CUM][:, 0:3 * CH], lower, kind[:, :, :].rearrange("p k m -> p (k m)"), start=True, stop=True)
            nc.tensor.matmul(bank[CUM][:, 3 * CH:6 * CH], all_ones, kind[:, :, :].rearrange("p k m -> p (k m)"),
                             start=True, stop=True).then_inc(s_cum, 1)
            def take(o, j, start, stop):
                pe.wait_ge(s_hot, j + 1)
                pe.wait_ge(s_picked, j + 1)
                for k in range(HG):
                    last = nc.tensor.matmul(bank[ROWS][:, 0:2 * TILES], is_lo[:, o, k, :],
                                            picked[:, o, k, :, :].rearrange("p v t -> p (v t)"),
                                            start=start and k == 0, stop=stop and k == HG - 1)
                last.then_inc(s_pick, 1)

            for j in range(CH // HG):
                take(j % SR, j, j == 0, j == CH // HG - 1)
            for v, where in ((0, PICK_ROW), (1, PICK_PSI)):
                pe.wait_ge(s_slot, v + 1)
                for g in range(QUADS):
                    last = nc.tensor.matmul(bank[where][:, g * TILES:(g + 1) * TILES],
                                            pick[:, g, :, :].rearrange("p q r -> p (q r)"),
                                            row_s[:, 0, :] if v == 0 else row_psi[:, :], start=True, stop=True)
                last.then_inc(s_quads, 1)

            pe.wait_ge(s_spread, 1)
            for q in range(QN // 512):
                last = nc.tensor.matmul(bank[SPREAD[q]][:, :], quad_ones,
                                        spread[:, 16 * q:16 * q + 16, :].rearrange("p m c -> p (m c)"), start=True, stop=True)
            last.then_inc(s_bc, 1)

            pe.wait_ge(s_low, STEPS + CREDIT["s_low"])
            pe.wait_ge(s_gl, 1)
            lists = list_ends(pe)

            def product(b, where, slot_, c, semaphore):
                for m in range(CH):
                    for a in range(2):
                        last = nc.tensor.matmul(acc[b][where][a][:, 0:FD], turned[:, slot_, m % PB, :, m // PB],
                                                tables[:, c, m, a, 0:FD], start=(m == 0), stop=(m == CH - 1))
                last.then_inc(semaphore, 1)

            def tile(T, b, what):
                pe.wait_ge(s_sum, T + (CREDIT["s_sum"] - 1))
                if what in ANY_MIXED:
                    wait_alone(pe, s_tfirst, T * 4 + 4)
                    product(b, 0, slot_of(b, what, PLUS), PLUS, s_mfirst)
                    wait_alone(pe, s_tlast, T * 4 + (4 + CREDIT["s_tlast"]))
                    product(b, 1, slot_of(b, what, MINUS), MINUS, s_mlast)
                else:
                    wait_alone(pe, s_tlast, T * 4 + (4 + CREDIT["s_tlast"]))
                    product(b, 0, b, PLUS if what == ONE_PLUS else MINUS, s_mlast)
                    pe.sem_inc(s_mfirst, 1)

            def pair(G):
                for b in range(2):
                    by_kind(pe, G * 2 + b, lists, lambda what: tile(G * 2 + b, b, what), True)

            with pe.If(lists[0] < STEPS):
                wait_alone(pe, s_tau, 1)
                wait_alone(pe, s_low, 2 * STEPS + CREDIT["s_low"])
                with pe.Fori(0, STEPS // 2) as G:
                    pair(G)
            with pe.Else():
                with pe.Fori(0, STEPS // 2) as G:
                    for b in range(2):
                        tile(G * 2 + b, b, ONE_PLUS)
            wait_alone(pe, s_tau, 1)
            wait_alone(pe, s_low, 2 * STEPS + CREDIT["s_low"])
            with pe.Fori(STEPS // 2, PAIRS) as G:
                pair(G)

def kernel(x, adj, L0_gnn_W1, L0_gnn_b1, L0_gnn_a1, L0_gnn_a2, L0_gnn_b2):
    import numpy as _np
    import concourse.bacc as _bacc
    from concourse import mybir as _mybir
    from concourse.bass_utils import run_bass_kernel_spmd as _run

    nc = _bacc.Bacc("TRN2", target_bir_lowering=False, num_devices=1, dynamic_dma_scratch_size=4096)
    given = {"x": x, "adj": adj, "w1": L0_gnn_W1, "b1": L0_gnn_b1, "a1": L0_gnn_a1, "a2": L0_gnn_a2, "b2": L0_gnn_b2}
    arrays, args = {}, []
    for name, value in given.items():
        a = _np.ascontiguousarray(value)
        if name == "b2":
            a = a.reshape(1)
        arrays[f"in_{name}"] = a
        args.append(nc.dram_tensor(f"in_{name}", a.shape, _mybir.dt.from_np(a.dtype), kind="ExternalInput").ap())
    out = nc.dram_tensor("out", given["x"].shape, F32, kind="ExternalOutput").ap()
    adjacency_attention(nc, *args, out)
    r = _run(nc, [arrays], core_ids=[0])
    return r.results[0]["out"]
```
